# Optimizing a Trainium2 kernel written in Bass

```python
import numpy as np
import jax
import jax.numpy as jnp

def _softmax(x, axis=-1):
    return jax.nn.softmax(x, axis=axis)

def _gelu(x):
    return jax.nn.gelu(x, approximate=True)

def _silu(x):
    return jax.nn.silu(x)

def _sigmoid(x):
    return jax.nn.sigmoid(x)

def _layernorm(x, axis=-1, eps=1e-05):
    m = jnp.mean(x, axis=axis, keepdims=True)
    v = jnp.var(x, axis=axis, keepdims=True)
    return (x - m) / jnp.sqrt(v + eps)

def _scatter_add(tgt, idx, src, axis=0):
    return tgt.at[idx].add(src)

def _segment_sum(src, seg, n):
    return jax.ops.segment_sum(src, seg, n)
kernel_name = 'mk_adj_seq_d2_adj_r2_b2ab8b'

def setup_inputs(seed: int=0):
    np.random.seed(seed)
    _w = jnp.asarray

    def _rec_inputs():
        import jax
        import jax.numpy as jnp
        _gk = jax.random.key(seed)
        x = 7.22e-05 + 1 * jax.random.normal(jax.random.fold_in(_gk, 1), (16, 512, 256), jnp.float32)
        _w = (1.0 + jnp.arange(512, dtype=jnp.float32)) ** (-0.5)
        _w = _w / _w.mean()
        _pij = jnp.clip(0.03125 * _w[:, None] * _w[None, :], 0.0, 1.0)
        _a = jax.random.uniform(jax.random.fold_in(_gk, 2), (16, 512, 512)) < _pij
        _af = _a.astype(jnp.float32)
        adj = _af
        return (x, adj)
    x, adj = _rec_inputs()

    def _L0_gnn_setup():
        import jax, jax.numpy as jnp
        import numpy as np
        import math
        EMBED = 256
        DFF = 256
        B, N = (8, 1024)
        key = jax.random.key(seed)
        ks = jax.random.split(key, 8)
        node_fts = jax.random.normal(ks[0], (B, N, EMBED), dtype=jnp.float32)
        rel_edges = jax.random.randint(ks[1], (B, N, N), 0, 2).astype(jnp.float32)
        s = 1.0 / math.sqrt(EMBED)
        Wq = jax.random.normal(ks[2], (EMBED, DFF), dtype=jnp.float32) * s
        bq = jnp.zeros((DFF,), dtype=jnp.float32)
        Wk = jax.random.normal(ks[3], (EMBED, DFF), dtype=jnp.float32) * s
        bk = jnp.zeros((DFF,), dtype=jnp.float32)
        Wc = jax.random.normal(ks[4], (EMBED, EMBED), dtype=jnp.float32) * s
        gamma = jnp.ones((EMBED,), dtype=jnp.float32)
        beta = jnp.zeros((EMBED,), dtype=jnp.float32)
        return {'node_fts': node_fts, 'rel_edges': rel_edges, 'Wq': Wq, 'bq': bq, 'Wk': Wk, 'bk': bk, 'Wc': Wc, 'gamma': gamma, 'beta': beta}
    _L0_gnn_all = _L0_gnn_setup()
    _L0_gnn_in = {k: v for k, v in _L0_gnn_all.items() if k in ('Wq', 'bq', 'Wk', 'bk', 'Wc', 'gamma', 'beta')}
    del _L0_gnn_all

    def _L1_gnn_setup():
        import jax, jax.numpy as jnp
        import numpy as np
        B, N, D, H = (8, 512, 256, 8)
        DK = D // H
        LN_EPS = 1e-05
        ADJ_MIN = 1e-08

        def _layer_norm(x, gamma, beta):
            mu = jnp.mean(x, axis=-1, keepdims=True)
            var = jnp.mean(jnp.square(x - mu), axis=-1, keepdims=True)
            return (x - mu) * jax.lax.rsqrt(var + LN_EPS) * gamma + beta
        key = jax.random.key(seed)
        ks = jax.random.split(key, 12)
        x = jax.random.normal(ks[0], (B, N, D), dtype=jnp.float32)
        adj = jax.random.uniform(ks[1], (B, N, N), dtype=jnp.float32)
        adj = adj / jnp.sum(adj, axis=-1, keepdims=True)
        s = 1.0 / np.sqrt(D)
        Wq = jax.random.normal(ks[2], (D, D), dtype=jnp.float32) * s
        bq = jnp.zeros((D,), dtype=jnp.float32)
        Wk = jax.random.normal(ks[3], (D, D), dtype=jnp.float32) * s
        bk = jnp.zeros((D,), dtype=jnp.float32)
        Wv = jax.random.normal(ks[4], (D, D), dtype=jnp.float32) * s
        bv = jnp.zeros((D,), dtype=jnp.float32)
        Wo = jax.random.normal(ks[5], (D, D), dtype=jnp.float32) * s
        bo = jnp.zeros((D,), dtype=jnp.float32)
        gamma = jnp.ones((D,), dtype=jnp.float32)
        beta = jnp.zeros((D,), dtype=jnp.float32)
        return {'x': x, 'adj': adj, 'Wq': Wq, 'bq': bq, 'Wk': Wk, 'bk': bk, 'Wv': Wv, 'bv': bv, 'Wo': Wo, 'bo': bo, 'gamma': gamma, 'beta': beta}
    _L1_gnn_all = _L1_gnn_setup()
    _L1_gnn_in = {k: v for k, v in _L1_gnn_all.items() if k in ('Wq', 'bq', 'Wk', 'bk', 'Wv', 'bv', 'Wo', 'bo', 'gamma', 'beta')}
    del _L1_gnn_all
    return {'x': x, 'adj': adj, 'L0_gnn_Wq': _L0_gnn_in['Wq'], 'L0_gnn_bq': _L0_gnn_in['bq'], 'L0_gnn_Wk': _L0_gnn_in['Wk'], 'L0_gnn_bk': _L0_gnn_in['bk'], 'L0_gnn_Wc': _L0_gnn_in['Wc'], 'L0_gnn_gamma': _L0_gnn_in['gamma'], 'L0_gnn_beta': _L0_gnn_in['beta'], 'L1_gnn_Wq': _L1_gnn_in['Wq'], 'L1_gnn_bq': _L1_gnn_in['bq'], 'L1_gnn_Wk': _L1_gnn_in['Wk'], 'L1_gnn_bk': _L1_gnn_in['bk'], 'L1_gnn_Wv': _L1_gnn_in['Wv'], 'L1_gnn_bv': _L1_gnn_in['bv'], 'L1_gnn_Wo': _L1_gnn_in['Wo'], 'L1_gnn_bo': _L1_gnn_in['bo'], 'L1_gnn_gamma': _L1_gnn_in['gamma'], 'L1_gnn_beta': _L1_gnn_in['beta']}

def reference(x, adj, L0_gnn_Wq, L0_gnn_bq, L0_gnn_Wk, L0_gnn_bk, L0_gnn_Wc, L0_gnn_gamma, L0_gnn_beta, L1_gnn_Wq, L1_gnn_bq, L1_gnn_Wk, L1_gnn_bk, L1_gnn_Wv, L1_gnn_bv, L1_gnn_Wo, L1_gnn_bo, L1_gnn_gamma, L1_gnn_beta):
    import jax
    import jax.numpy as jnp

    def _L0_gnn_ref(node_fts, rel_edges, Wq, bq, Wk, bk, Wc, gamma, beta):
        import jax, jax.numpy as jnp
        import numpy as np
        import math
        EMBED = 256
        DFF = 256
        B, N = (8, 1024)
        denom = math.sqrt(DFF)
        q = node_fts @ Wq + bq
        k = node_fts @ Wk + bk
        scores = jnp.einsum('bod,bid->boi', q, k) / denom
        mask = rel_edges == 0
        scores = jnp.where(mask, -1e+18, scores)
        attn = jax.nn.softmax(scores, axis=2)
        attn = jnp.where(mask, 0.0, attn)
        ctx = jnp.einsum('boi,bie->boe', attn, node_fts) @ Wc
        x = node_fts + ctx
        mu = jnp.mean(x, axis=-1, keepdims=True)
        var = jnp.mean(jnp.square(x - mu), axis=-1, keepdims=True)
        out = (x - mu) * jax.lax.rsqrt(var + 1e-05) * gamma + beta
        return out

    def _L1_gnn_ref(x, adj, Wq, bq, Wk, bk, Wv, bv, Wo, bo, gamma, beta):
        import jax, jax.numpy as jnp
        import numpy as np
        B, N, D, H = (8, 512, 256, 8)
        DK = D // H
        LN_EPS = 1e-05
        ADJ_MIN = 1e-08

        def _layer_norm(x, gamma, beta):
            mu = jnp.mean(x, axis=-1, keepdims=True)
            var = jnp.mean(jnp.square(x - mu), axis=-1, keepdims=True)
            return (x - mu) * jax.lax.rsqrt(var + LN_EPS) * gamma + beta
        b, n, d = x.shape
        q = (x @ Wq.T + bq).reshape(b, n, H, DK).transpose(0, 2, 1, 3)
        k = (x @ Wk.T + bk).reshape(b, n, H, DK).transpose(0, 2, 1, 3)
        v = (x @ Wv.T + bv).reshape(b, n, H, DK).transpose(0, 2, 1, 3)
        logits = jnp.einsum('bhqd,bhkd->bhqk', q, k) / np.sqrt(DK)
        logits = logits + jnp.log(jnp.clip(adj, ADJ_MIN, None))[:, None, :, :]
        attn = jax.nn.softmax(logits, axis=-1)
        out = jnp.einsum('bhqk,bhkd->bhqd', attn, v)
        out = out.transpose(0, 2, 1, 3).reshape(b, n, d)
        out = out @ Wo.T + bo
        return _layer_norm(x + out, gamma, beta)
    x = _L0_gnn_ref(x, adj, L0_gnn_Wq, L0_gnn_bq, L0_gnn_Wk, L0_gnn_bk, L0_gnn_Wc, L0_gnn_gamma, L0_gnn_beta)
    x = _L1_gnn_ref(x, adj, L1_gnn_Wq, L1_gnn_bq, L1_gnn_Wk, L1_gnn_bk, L1_gnn_Wv, L1_gnn_bv, L1_gnn_Wo, L1_gnn_bo, L1_gnn_gamma, L1_gnn_beta)
    return x

_drawn_inputs = setup_inputs


def setup_inputs(seed=0):
    import zlib

    import numpy as np

    out = dict(_drawn_inputs(seed))
    spreads = {'L0_gnn_bq': (0.0, 0.1),
     'L0_gnn_bk': (0.0, 0.1),
     'L0_gnn_gamma': (1.0, 0.2),
     'L0_gnn_beta': (0.0, 0.1),
     'L1_gnn_bq': (0.0, 0.1),
     'L1_gnn_bk': (0.0, 0.1),
     'L1_gnn_bv': (0.0, 0.1),
     'L1_gnn_bo': (0.0, 0.1),
     'L1_gnn_gamma': (1.0, 0.2),
     'L1_gnn_beta': (0.0, 0.1)}
    factors = {}
    for name, (base, spread) in spreads.items():
        noise = np.random.default_rng([zlib.crc32(name.encode()), seed]).standard_normal(out[name].shape)
        drawn = base * np.exp(spread * noise) if base else spread * noise
        out[name] = jnp.asarray(drawn.astype(out[name].dtype))
    for name, factor in factors.items():
        out[name] = (out[name] * factor).astype(out[name].dtype)
    return out
```

```python
from contextlib import ExitStack

import concourse.bass as bass
from concourse import mybir

F32 = mybir.dt.float32
F32R = mybir.dt.float32r
BF16 = mybir.dt.bfloat16
ALU = mybir.AluOpType
ACT = mybir.ActivationFunctionType
AX = mybir.AxisListType

P = 128
HEADS = 8
PER_GROUP = 4
GROUPS = HEADS // PER_GROUP
MASKED = -1e18
MAX_FLOOR = -1e17
ADJ_MIN = 1e-8
LN_EPS = 1e-5
TINY = 1e-30
DMA = 16


class Phase:

    def __init__(self, kind, i, j):
        self.kind, self.i, self.j = kind, i, j
        self.front, self.back = kind != "last", kind != "first"


def misc_order(tiles):
    A, D = "act", "dve"
    max_back = [(f"max1_1_{n}", D) for n in range(4 * tiles)]
    max_front = [(f"max1_0_{n}", D) for n in range(4 * tiles)]
    return (
        [("v_0", A), ("v_1", A), ("q0_0", D), ("q0_1", D), ("k0_0", D), ("k0_1", D)] + max_back[0:4]
        + [("u_0", A), ("u_1", A)] + max_back[4:8] + [("max0_0", D), ("max0_1", D)]
        + max_back[8:12] + [("max0_2", D), ("max0_3", D)]
        + max_back[12:16] + [("mrow1_1", D), None, ("mrow0", D), ("exp0_0", A), ("exp0_1", A)]
        + [("exp0_2", A), ("exp0_3", A), ("ctx_0", D), ("ctx_1", D)]
        + [("ctx_2", D), ("ctx_3", D)]
        + [("tr_0", A), ("tr_1", A), ("q1_0", D), ("k1_0", D)]
        + max_front[0:8] + [("q1_1", D), ("k1_1", D)]
        + max_front[8:16] + [("mrow1_0", D)]
    )


def is_back(name):
    return name.startswith(("v_", "max1_1", "mrow1_1"))


class MiscBanks:

    def __init__(self, order, graphs):
        self.order = {
            "first": [u for u in order if u and not is_back(u[0])],
            "steady": order,
            "last": [u for u in order if u and is_back(u[0])],
        }
        assert all(len(self.order[k]) % 2 == 0 for k in ("first", "steady"))
        self.graphs = graphs

    def _count(self, kind, what):
        return sum(1 for u in self.order[kind] if u and what in ("fill", u[1]))

    def _base(self, ph, what):
        first, steady = self._count("first", what), self._count("steady", what)
        if ph.kind == "first":
            return 0
        if ph.kind == "steady":
            return ph.i * steady + first
        return (self.graphs - 1) * steady + first

    def _index(self, ph, name):
        return next(n for n, u in enumerate(self.order[ph.kind]) if u and u[0] == name)

    def bank(self, ph, name):
        return self._index(ph, name) % 2

    def engine(self, name):
        return next(u[1] for u in self.order["steady"] if u and u[0] == name)

    def count(self, ph, name, what):
        uses = self.order[ph.kind][: self._index(ph, name) + 1]
        return self._base(ph, what) + sum(1 for u in uses if u and what in ("fill", u[1]))

    def count_before(self, ph, name):
        order, e = self.order["steady"], self.engine(name)
        n = next(n for n, u in enumerate(order) if u and u[0] == name)
        assert not any(is_back(u[0]) for u in order[n:] if u)
        return self._base(ph, e) - sum(1 for u in order[n + 1:] if u and u[1] == e)

    def before(self, ph, name):
        n = self._index(ph, name) - 2
        uses = self.order[ph.kind]
        while n >= 0 and uses[n] is None:
            n -= 2
        if n >= 0:
            return uses[n][1], self.count(ph, uses[n][0], uses[n][1])
        if ph.kind == "first":
            return None
        uses = self.order["steady"]
        assert uses[n] is not None
        later = sum(1 for u in uses[len(uses) + n + 1:] if u and u[1] == uses[n][1])
        return uses[n][1], self._base(ph, uses[n][1]) - later


COLS = ("L0_gnn_bq", "L0_gnn_bk", "L1_gnn_bq", "L1_gnn_bk", "L1_gnn_bv", "L0_gnn_gamma", "L0_gnn_beta")
ROWS = ("L0_gnn_gamma", "L0_gnn_beta", "L1_gnn_bo", "L1_gnn_gamma", "L1_gnn_beta")


def two_layer_graph_attention(nc, x, x_t, adj_t, wq0, wk0, wc0, wq1_t, wk1_t, wv1_t, wo1_t,
                              channel_cols, channel_rows, out):
    B, N, D = x.shape
    T = N // P
    C = D // P
    DK = D // HEADS
    SCALE0 = float(D) ** -0.5
    SCALE1 = float(DK) ** -0.5
    assert (T, C, DK, GROUPS) == (4, 2, 32, C) and HEADS * DK == D
    HI_HI, HI_LO, LO_HI, MROW = 0, DK, 2 * DK, 3 * DK
    STACK = 3 * DK + 1
    UNITS = GROUPS * T * 2
    QUADS = GROUPS * T
    STACK_DMAS = 6 * PER_GROUP

    misc = MiscBanks(misc_order(T), B)
    PRE = Phase("first", None, 0)
    POST = Phase("last", B - 1, None)

    with ExitStack() as ctx:
        def sb(name, shape, dt=F32):
            return ctx.enter_context(nc.sbuf_tensor(name, shape, dt))

        def ps(name, shape):
            return ctx.enter_context(nc.psum_tensor(name, shape, F32))

        def sem(name):
            return ctx.enter_context(nc.semaphore(name))

        ident = sb("ident", [P, P])
        ident_bf = sb("ident_bf", [P, P], BF16)
        ones = sb("ones", [P, P])
        ones_r = sb("ones_r", [1, P], F32R)
        minus_half = sb("minus_half", [P, T])
        eps = sb("eps", [P, T])
        scratch = sb("scratch", [P, 1])
        Wq0, Wk0, Wc0 = (sb(n, [P, C, D]) for n in ("Wq0", "Wk0", "Wc0"))
        Wq1, Wk1, Wv1, Wo1 = (sb(n, [P, C, D]) for n in ("Wq1", "Wk1", "Wv1", "Wo1"))
        cols = sb("cols", [P, len(COLS), C])
        BQ0, BK0, BQ1, BK1, BV1, G0, B0 = range(len(COLS))
        rows = sb("rows", [1, len(ROWS), D])
        R_G0, R_B0, R_BO, R_G1, R_B1 = range(len(ROWS))
        bv_wide = sb("bv_wide", [P, C, P])
        spread = sb("spread", [P, 4, D])
        S_G0, S_RES, S_G1, S_B1 = range(4)

        X = sb("X", [P, T, D])
        XT = sb("XT", [P, C, N])
        ADJ = sb("ADJ", [P, T, N])
        BIAS = sb("BIAS", [P, T, N], BF16)
        Q0H, Q0L, K0H, K0L = (sb(n, [P, C, N], F32R) for n in ("Q0H", "Q0L", "K0H", "K0L"))
        U = sb("U", [P, T, D + 1])
        mx0 = sb("mx0", [P, T])
        nm0 = sb("nm0", [1, N], F32R)
        P0 = sb("P0", [P, T, N])
        den0 = sb("den0", [P, T])
        rden0 = sb("rden0", [P, T])
        xr = sb("xr", [P, T, D])
        st0 = sb("st0", [P, T, 6])
        mv0 = sb("mv0", [P, T, 2])
        ve0 = sb("ve0", [P, T])
        rstd0 = sb("rstd0", [P, T])
        xn = sb("xn", [P, T, D])
        X1T = sb("X1T", [P, C, N])
        Q1H, Q1L, K1H, K1L = (sb(n, [P, C, N], F32R) for n in ("Q1H", "Q1L", "K1H", "K1L"))
        mx1 = sb("mx1", [P, GROUPS, T, PER_GROUP])
        nm1 = [sb(f"nm1_{g}", [PER_GROUP, N], F32R) for g in range(GROUPS)]
        QS = sb("QS", [STACK, HEADS, N], F32R)
        KS = sb("KS", [STACK, HEADS, N], F32R)

        V = sb("V", [P, T, D])
        CLIP = sb("CLIP", [P, T, N])
        PR = [sb(f"PR{n}", [P, PER_GROUP, N]) for n in range(2)]
        rden1 = sb("rden1", [P, N])
        OT = sb("OT", [P, C, N])
        res = sb("res", [P, T, D])
        z = sb("z", [P, T, D])
        st1 = sb("st1", [P, T, 6])
        mv1 = sb("mv1", [P, T, 2])
        ve1 = sb("ve1", [P, T])
        rstd1 = sb("rstd1", [P, T])
        zn = sb("zn", [P, T, D])
        og = sb("og", [P, T, D])

        MISC = [ps(f"misc{n}", [P, N]) for n in range(2)]
        ST = [ps(f"scores{n}", [P, 2, N]) for n in range(2)]
        PV = ps("values", [P, N])
        DEN = ps("denominators", [P, N])

        weights_loaded = sem("weights_loaded")
        consts_set = sem("consts_set")
        ident_zeroed = sem("ident_zeroed")
        ident_ready = sem("ident_ready")
        bv_widened = sem("bv_widened")
        spread_filled = sem("spread_filled")
        spread_ready = sem("spread_ready")
        x_loaded = sem("x_loaded")
        xt_loaded = sem("xt_loaded")
        adj_loaded = sem("adj_loaded")
        misc_filled = sem("misc_filled")
        misc_drained = {"act": sem("misc_drained_act"), "dve": sem("misc_drained_dve")}
        hi_written = sem("hi_written")
        bias_built = sem("bias_built")
        adj_clipped = sem("adj_clipped")
        front_step = sem("front_step")
        back_step = sem("back_step")
        stats0_ready = sem("stats0_ready")
        rstd0_ready = sem("rstd0_ready")
        xn_ready = sem("xn_ready")
        pool_step0 = sem("pool_step0")
        pool_step1 = sem("pool_step1")
        stack_loaded = [sem(f"stack_loaded{g}") for g in range(GROUPS)]
        mrow_loaded = [sem(f"mrow_loaded{g}") for g in range(GROUPS)]
        scores_filled = sem("scores_filled")
        exp_done = sem("exp_done")
        masked = sem("masked")
        quad_summed = sem("quad_summed")
        normalised = sem("normalised")
        proj_filled = sem("proj_filled")
        z_added = sem("z_added")
        stats1_ready = sem("stats1_ready")
        rstd1_ready = sem("rstd1_ready")
        zn_ready = sem("zn_ready")
        res_ready = sem("res_ready")
        out_ready = sem("out_ready")
        out_stored = sem("out_stored")

        LOADS = 7 + 2
        block = ctx.enter_context(nc.Block())

        def wait_drained(eng, ph, name):
            e = misc.engine(name)
            eng.wait_ge(misc_drained[e], misc.count(ph, name, e))

        def wait_filled(eng, ph, name):
            eng.wait_ge(misc_filled, misc.count(ph, name, "fill"))

        def run(eng, step):
            step(PRE)
            with eng.Fori(0, B - 1) as i:
                step(Phase("steady", i, i + 1))
            step(POST)

        @block.sync
        def _(sp):
            for w, src in ((Wq0, wq0), (Wk0, wk0), (Wc0, wc0), (Wq1, wq1_t), (Wk1, wk1_t),
                           (Wv1, wv1_t), (Wo1, wo1_t)):
                sp.dma_start(w[:], src.rearrange("(c p) e -> p c e", p=P)).then_inc(weights_loaded, DMA)
            sp.dma_start(cols[:], channel_cols).then_inc(weights_loaded, DMA)
            sp.dma_start(rows[:], channel_rows).then_inc(weights_loaded, DMA)

            def load_stacks(g):
                for h in range(PER_GROUP):
                    part = slice(DK * h, DK * (h + 1))
                    for stack, parts in ((QS, (Q1H, Q1H, Q1L)), (KS, (K1H, K1L, K1H))):
                        for row, src in zip((HI_HI, HI_LO, LO_HI), parts):
                            sp.dma_start(stack[row:row + DK, PER_GROUP * g + h, :].bitcast(F32),
                                         src[part, g, :].bitcast(F32)).then_inc(stack_loaded[g], DMA)

            def load_mrow(g):
                sp.dma_start(QS[MROW:STACK, PER_GROUP * g:PER_GROUP * (g + 1), :].bitcast(F32),
                             nm1[g][:].bitcast(F32)).then_inc(mrow_loaded[g], DMA)

            def step(ph):
                i, j = ph.i, ph.j
                if ph.front:
                    if ph.back:
                        sp.wait_ge(xn_ready, i * T + T)
                    sp.dma_start(X[:], x[j].rearrange("(t p) e -> p t e", p=P)).then_inc(x_loaded, DMA)
                    if ph.back:
                        sp.wait_ge(adj_clipped, i + 1)
                    sp.dma_start(ADJ[:], adj_t[j].rearrange("(t p) q -> p t q", p=P)).then_inc(adj_loaded, DMA)
                if ph.back:
                    wait_drained(sp, ph, "mrow1_1")
                    load_mrow(1)
                if ph.front:
                    wait_drained(sp, ph, "k1_0")
                    load_stacks(0)
                    wait_drained(sp, ph, "k1_1")
                    load_stacks(1)
                    wait_drained(sp, ph, "mrow1_0")
                    load_mrow(0)
                if ph.back:
                    sp.wait_ge(out_ready, i + 1)
                    sp.dma_start(out[i].rearrange("(t p) e -> p t e", p=P), og[:]).then_inc(out_stored, DMA)

            run(sp, step)
            sp.wait_ge(out_stored, B * DMA + 1)

        @block.tensor
        def _(pe):
            def fill(ph, name):
                before = misc.before(ph, name)
                if before is not None:
                    pe.wait_ge(misc_drained[before[0]], before[1])
                return MISC[misc.bank(ph, name)]

            pe.wait_ge(weights_loaded, LOADS * DMA)
            pe.wait_ge(consts_set, 7)
            pe.wait_ge(ident_ready, 2)
            pe.wait_ge(bv_widened, C)
            one = ones[0:1, :]
            pe.matmul(ST[0][:, 0, 0:D], one, rows[:, R_G0, :], start=True, stop=True)
            for n in (R_B0, R_BO):
                pe.matmul(ST[0][:, 1, 0:D], one, rows[:, n, :], start=(n == R_B0), stop=False)
            for c in range(C):
                pe.matmul(ST[0][:, 1, 0:D], bv_wide[:, c, :], Wo1[:, c, :], start=False, stop=(c == C - 1))
            pe.matmul(ST[1][:, 0, 0:D], one, rows[:, R_G1, :], start=True, stop=True)
            pe.matmul(ST[1][:, 1, 0:D], one, rows[:, R_B1, :], start=True, stop=True).then_inc(spread_filled, 1)

            def project(ph, name, weights, src, c):
                bank = fill(ph, name)
                for k in range(C):
                    mm = pe.matmul(bank[:], weights[:, k, P * c:P * (c + 1)], src[:, k, :],
                                   start=(k == 0), stop=(k == C - 1))
                mm.then_inc(misc_filled, 1)

            def project_rows(ph, name, weights, src, n):
                bank = fill(ph, name)
                for half in range(2):
                    t = 2 * n + half
                    for k in range(C):
                        mm = pe.matmul(bank[:, D * half:D * (half + 1)], src[:, k, P * t:P * (t + 1)],
                                       weights[:, k, :], start=(k == 0), stop=(k == C - 1))
                mm.then_inc(misc_filled, 1)

            def max0(ph, t):
                if t == 0:
                    wait_drained(pe, ph, "k0_1")
                    pe.wait_ge(bias_built, ph.j + 1)
                bank = fill(ph, f"max0_{t}")
                q = slice(P * t, P * (t + 1))
                for c in range(C):
                    pe.matmul(bank[:], Q0H[:, c, q], K0H[:, c, :], start=(c == 0), stop=False)
                for k in range(T):
                    mm = pe.matmul(bank[:, P * k:P * (k + 1)], BIAS[:, k, q], ident_bf[:],
                                   start=False, stop=(k == T - 1))
                mm.then_inc(misc_filled, 1)

            def mrow0(ph):
                wait_drained(pe, ph, "max0_3")
                bank = fill(ph, "mrow0")
                for t in range(T):
                    mm = pe.matmul(bank[0:1, P * t:P * (t + 1)], mx0[:, t:t + 1], ident[:],
                                   start=True, stop=True)
                mm.then_inc(misc_filled, 1)

            def scores0(ph, k):
                if k == 0:
                    wait_drained(pe, ph, "mrow0")
                bank = fill(ph, f"exp0_{k}")
                rows_k = slice(P * k, P * (k + 1))
                n = 0
                for c in range(C):
                    for kk, qq in ((K0H, Q0H), (K0L, Q0H), (K0H, Q0L)):
                        pe.matmul(bank[:], kk[:, c, rows_k], qq[:, c, :], start=(n == 0), stop=False)
                        n += 1
                pe.matmul(bank[:], ones_r[:], nm0[:], start=False, stop=False)
                pe.matmul(bank[:], ident_bf[:], BIAS[:, k, :], start=False, stop=True).then_inc(misc_filled, 1)

            def context0(ph, t):
                if t == 0:
                    wait_drained(pe, ph, "exp0_3")
                    wait_drained(pe, ph, "u_1")
                bank = fill(ph, f"ctx_{t}")
                for k in range(T):
                    mm = pe.matmul(bank[:, 0:D + 1], P0[:, k, P * t:P * (t + 1)], U[:, k, :],
                                   start=(k == 0), stop=(k == T - 1))
                mm.then_inc(misc_filled, 1)

            def transpose_x1(ph, c):
                if c == 0:
                    pe.wait_ge(xn_ready, ph.j * T + T)
                bank = fill(ph, f"tr_{c}")
                for t in range(T):
                    mm = pe.transpose(bank[:, P * t:P * (t + 1)], xn[:, t, P * c:P * (c + 1)], ident[:])
                mm.then_inc(misc_filled, 1)

            def max1(ph, g, first, last):
                if g == 0:
                    wait_drained(pe, ph, "k1_0")
                else:
                    pe.wait_ge(misc_drained["dve"], misc.count_before(ph, "k1_1"))
                for n in range(first, last):
                    bank = fill(ph, f"max1_{g}_{n}")
                    t, h = divmod(n, PER_GROUP)
                    part = slice(DK * h, DK * (h + 1))
                    pe.matmul(bank[:], Q1H[part, g, P * t:P * (t + 1)], K1H[part, g, :],
                              start=True, stop=True).then_inc(misc_filled, 1)

            def mrow1(ph, g):
                wait_drained(pe, ph, f"max1_{g}_{4 * T - 1}")
                bank = fill(ph, f"mrow1_{g}")
                for t in range(T):
                    mm = pe.matmul(bank[0:PER_GROUP, P * t:P * (t + 1)], mx1[:, g, t, :], ident[:],
                                   start=True, stop=True)
                mm.then_inc(misc_filled, 1)

            def scores1(ph, quad):
                g, k = divmod(quad, T)
                for pair in range(2):
                    if k == 0 and pair == 0:
                        pe.wait_ge(stack_loaded[g], (ph.i + 1) * (STACK_DMAS * DMA))
                        pe.wait_ge(mrow_loaded[g], (ph.i + 1) * DMA)
                    if quad:
                        pe.wait_ge(exp_done, ph.i * UNITS + 2 * (quad - 1) + pair + 1)
                    for n in range(2):
                        h = PER_GROUP * g + 2 * pair + n
                        mm = pe.matmul(ST[pair][:, n, :], KS[:, h, P * k:P * (k + 1)], QS[:, h, :],
                                       start=True, stop=True)
                    mm.then_inc(scores_filled, 1)

            def values1(ph, quad):
                g, k = divmod(quad, T)
                pe.wait_ge(masked, ph.i * UNITS + 2 * quad + 2)
                if quad == 0:
                    wait_drained(pe, ph, "v_1")
                elif k == 0:
                    pe.wait_ge(normalised, ph.i * GROUPS + g)
                for bank, what in ((PV, V), (DEN, ones)):
                    for h in range(PER_GROUP):
                        c = DK * (PER_GROUP * g + h)
                        w = V[:, k, c:c + DK] if what is V else ones[:, 0:DK]
                        mm = pe.matmul(bank[DK * h:DK * (h + 1), :], w, PR[quad % 2][:, h, :],
                                       start=(k == 0), stop=(k == T - 1))
                mm.then_inc(quad_summed, 1)

            def project_out(ph):
                pe.wait_ge(normalised, ph.i * GROUPS + GROUPS)
                for t in range(T):
                    bank = (PV, DEN)[t // 2]
                    for c in range(C):
                        mm = pe.matmul(bank[:, D * (t % 2):D * (t % 2 + 1)], OT[:, c, P * t:P * (t + 1)],
                                       Wo1[:, c, :], start=(c == 0), stop=(c == C - 1))
                    if t % 2:
                        mm.then_inc(proj_filled, 1)

            def step(ph):
                f, b = ph.front, ph.back
                if b:
                    project_rows(ph, "v_0", Wv1, X1T, 0)
                    project_rows(ph, "v_1", Wv1, X1T, 1)
                if f:
                    pe.wait_ge(xt_loaded, ph.j * DMA + DMA)
                    project(ph, "q0_0", Wq0, XT, 0)
                    project(ph, "q0_1", Wq0, XT, 1)
                if b:
                    scores1(ph, 0)
                if f:
                    project(ph, "k0_0", Wk0, XT, 0)
                    project(ph, "k0_1", Wk0, XT, 1)
                if b:
                    max1(ph, 1, 0, 4)
                    scores1(ph, 1)
                    values1(ph, 0)
                if f:
                    project_rows(ph, "u_0", Wc0, XT, 0)
                    project_rows(ph, "u_1", Wc0, XT, 1)
                if b:
                    max1(ph, 1, 4, 8)
                if f:
                    max0(ph, 0)
                    max0(ph, 1)
                if b:
                    scores1(ph, 2)
                    values1(ph, 1)
                    max1(ph, 1, 8, 12)
                if f:
                    max0(ph, 2)
                    max0(ph, 3)
                if b:
                    scores1(ph, 3)
                    max1(ph, 1, 12, 16)
                    mrow1(ph, 1)
                    values1(ph, 2)
                if f:
                    mrow0(ph)
                    scores0(ph, 0)
                    scores0(ph, 1)
                if b:
                    values1(ph, 3)
                if f:
                    scores0(ph, 2)
                    scores0(ph, 3)
                if b:
                    scores1(ph, 4)
                if f:
                    context0(ph, 0)
                    context0(ph, 1)
                if b:
                    scores1(ph, 5)
                if f:
                    context0(ph, 2)
                    context0(ph, 3)
                if b:
                    values1(ph, 4)
                    scores1(ph, 6)
                    values1(ph, 5)
                if f:
                    transpose_x1(ph, 0)
                    transpose_x1(ph, 1)
                    wait_drained(pe, ph, "tr_1")
                    project(ph, "q1_0", Wq1, X1T, 0)
                    project(ph, "k1_0", Wk1, X1T, 0)
                if b:
                    scores1(ph, 7)
                if f:
                    max1(ph, 0, 0, 8)
                if b:
                    values1(ph, 6)
                if f:
                    project(ph, "q1_1", Wq1, X1T, 1)
                    project(ph, "k1_1", Wk1, X1T, 1)
                if b:
                    values1(ph, 7)
                if f:
                    max1(ph, 0, 8, 14)
                if b:
                    project_out(ph)
                if f:
                    max1(ph, 0, 14, 16)
                    mrow1(ph, 0)

            run(pe, step)

        @block.scalar
        def _(act):
            act.wait_ge(weights_loaded, LOADS * DMA)
            act.wait_ge(spread_filled, 1)
            for n in range(4):
                act.copy(spread[:, n, :], ST[n // 2][:, n % 2, 0:D]).then_inc(spread_ready, 1)

            def hi(ph, name, dst, c, bias):
                wait_filled(act, ph, name)
                act.activation(dst[:, c, :], MISC[misc.bank(ph, name)][:], ACT.Identity,
                               bias=cols[:, bias, c:c + 1]).then_inc(hi_written, 1)

            def rows_out(ph, name, dst, n):
                wait_filled(act, ph, name)
                act.copy(dst[:, 2 * n:2 * n + 2, 0:D],
                         MISC[misc.bank(ph, name)][:].rearrange("p (t e) -> p t e", t=2)).then_inc(misc_drained["act"], 1)

            def exp0(ph, k):
                wait_filled(act, ph, f"exp0_{k}")
                act.activation(P0[:, k, :], MISC[misc.bank(ph, f"exp0_{k}")][:], ACT.Exp,
                               scale=SCALE0).then_inc(misc_drained["act"], 1)

            def exp1(ph, quad):
                for pair in range(2):
                    unit = 2 * quad + pair
                    act.wait_ge(scores_filled, ph.i * UNITS + unit + 1)
                    if quad >= 2:
                        act.wait_ge(quad_summed, ph.i * QUADS + quad - 1)
                    act.activation(PR[quad % 2][:, 2 * pair:2 * pair + 2, :], ST[pair][:], ACT.Exp,
                                   scale=SCALE1).then_inc(exp_done, 1)

            def x1_out(ph, c):
                wait_filled(act, ph, f"tr_{c}")
                act.activation(X1T[:, c, :], MISC[misc.bank(ph, f"tr_{c}")][:], ACT.Identity,
                               scale=cols[:, G0, c:c + 1],
                               bias=cols[:, B0, c:c + 1]).then_inc(misc_drained["act"], 1)

            def step(ph):
                f, b = ph.front, ph.back
                if f:
                    act.dma_start(XT[:], x_t[ph.j].rearrange("(c p) n -> p c n", p=P)).then_inc(xt_loaded, DMA)
                if b:
                    rows_out(ph, "v_0", V, 0)
                    rows_out(ph, "v_1", V, 1)
                if f:
                    hi(ph, "q0_0", Q0H, 0, BQ0)
                    hi(ph, "q0_1", Q0H, 1, BQ0)
                if b:
                    exp1(ph, 0)
                if f:
                    hi(ph, "k0_0", K0H, 0, BK0)
                    hi(ph, "k0_1", K0H, 1, BK0)
                if b:
                    exp1(ph, 1)
                if f:
                    rows_out(ph, "u_0", U, 0)
                    rows_out(ph, "u_1", U, 1)
                if b:
                    exp1(ph, 2)
                    exp1(ph, 3)
                if f:
                    for k in range(T):
                        exp0(ph, k)
                if b:
                    exp1(ph, 4)
                    exp1(ph, 5)
                    exp1(ph, 6)
                if f:
                    x1_out(ph, 0)
                    x1_out(ph, 1)
                    hi(ph, "q1_0", Q1H, 0, BQ1)
                    hi(ph, "k1_0", K1H, 0, BK1)
                if b:
                    exp1(ph, 7)
                if f:
                    hi(ph, "q1_1", Q1H, 1, BQ1)
                    hi(ph, "k1_1", K1H, 1, BK1)

            run(act, step)

        @block.vector
        def _(dve):
            FRONT_STEPS = 2 * T + T
            BACK_STEPS = GROUPS + T

            dve.memset(ones[:], 1.0).then_inc(consts_set, 1)
            dve.memset(ones_r[:].bitcast(F32), 1.0).then_inc(consts_set, 1)
            dve.memset(minus_half[:], -0.5).then_inc(consts_set, 1)
            dve.memset(eps[:], LN_EPS).then_inc(consts_set, 1)
            dve.memset(U[:, :, D:D + 1], 1.0).then_inc(consts_set, 1)
            dve.memset(KS[MROW:STACK, :, :].bitcast(F32), 1.0).then_inc(consts_set, 1)
            dve.memset(bv_wide[:], 0.0).then_inc(consts_set, 1)
            dve.wait_ge(consts_set, 7)
            dve.wait_ge(ident_ready, 1)
            dve.tensor_copy(ident_bf[:], ident[:]).then_inc(ident_ready, 1)
            dve.wait_ge(weights_loaded, LOADS * DMA)
            for c in range(C):
                dve.tensor_scalar(bv_wide[:, c, :], bv_wide[:, c, :], cols[:, BV1, c:c + 1], None,
                                  ALU.add).then_inc(bv_widened, 1)

            def lo(ph, name, dst, hi_part, c, bias, nth):
                wait_filled(dve, ph, name)
                dve.wait_ge(hi_written, ph.j * 8 + nth + 1)
                dve.scalar_tensor_tensor(out=dst[:, c, :], in0=MISC[misc.bank(ph, name)][:],
                                         scalar=cols[:, bias, c:c + 1], in1=hi_part[:, c, :].bitcast(F32),
                                         op0=ALU.add, op1=ALU.subtract).then_inc(misc_drained["dve"], 1)

            def clip(ph):
                dve.wait_ge(adj_loaded, ph.i * DMA + DMA)
                dve.tensor_scalar(CLIP[:], ADJ[:], ADJ_MIN, None, ALU.max).then_inc(adj_clipped, 1)

            def bias(ph):
                dve.wait_ge(adj_loaded, ph.j * DMA + DMA)
                dve.tensor_scalar(BIAS[:], ADJ[:], 0.0, MASKED, ALU.is_equal, ALU.mult).then_inc(bias_built, 1)

            def max0(ph, t):
                wait_filled(dve, ph, f"max0_{t}")
                dve.tensor_reduce(mx0[:, t:t + 1], MISC[misc.bank(ph, f"max0_{t}")][:], AX.X,
                                  ALU.max).then_inc(misc_drained["dve"], 1)

            def mrow0(ph):
                wait_filled(dve, ph, "mrow0")
                dve.tensor_scalar(nm0[:], MISC[misc.bank(ph, "mrow0")][0:1, :], MAX_FLOOR, -1.0, ALU.max,
                                  ALU.mult).then_inc(misc_drained["dve"], 1)

            def max1(ph, g, first, last):
                for n in range(first, last):
                    t, h = divmod(n, PER_GROUP)
                    wait_filled(dve, ph, f"max1_{g}_{n}")
                    dve.tensor_reduce(mx1[:, g, t, h:h + 1], MISC[misc.bank(ph, f"max1_{g}_{n}")][:], AX.X,
                                      ALU.max, negate=True).then_inc(misc_drained["dve"], 1)

            def mrow1(ph, g):
                wait_filled(dve, ph, f"mrow1_{g}")
                dve.tensor_copy(nm1[g][:], MISC[misc.bank(ph, f"mrow1_{g}")][0:PER_GROUP, :])\
                   .then_inc(misc_drained["dve"], 1)

            def context0(ph, t):
                base = ph.j * FRONT_STEPS
                bank = MISC[misc.bank(ph, f"ctx_{t}")]
                wait_filled(dve, ph, f"ctx_{t}")
                if t == 0:
                    dve.wait_ge(x_loaded, ph.j * DMA + DMA)
                dve.tensor_scalar(den0[:, t:t + 1], bank[:, D:D + 1], TINY, None, ALU.max).then_inc(front_step, 1)
                dve.wait_ge(front_step, base + 2 * t + 1)
                dve.reciprocal(rden0[:, t:t + 1], den0[:, t:t + 1]).then_inc(front_step, 1)
                dve.wait_ge(front_step, base + 2 * t + 2)
                dve.scalar_tensor_tensor(out=xr[:, t, :], in0=bank[:, 0:D], scalar=rden0[:, t:t + 1],
                                         in1=X[:, t, :], op0=ALU.mult, op1=ALU.add)\
                   .then_inc(misc_drained["dve"], 1)

            def norm0(ph):
                base = ph.j * FRONT_STEPS + 2 * T
                for t in range(T):
                    wait_drained(dve, ph, f"ctx_{t}")
                    dve.bn_stats(st0[:, t, :], xr[:, t, :]).then_inc(front_step, 1)
                dve.wait_ge(front_step, base + T)
                dve.memset(scratch[:], 0.0)
                for t in range(T):
                    dve.bn_aggr(mv0[:, t, :], st0[:, t, :]).then_inc(stats0_ready, 1)
                dve.wait_ge(rstd0_ready, ph.j + 1)
                if ph.back:
                    dve.wait_ge(res_ready, ph.i + 1)
                for t in range(T):
                    dve.tensor_scalar(xn[:, t, :], xr[:, t, :], mv0[:, t, 0:1], rstd0[:, t:t + 1],
                                      ALU.subtract, ALU.mult).then_inc(xn_ready, 1)

            def normalise(ph, g):
                dve.wait_ge(quad_summed, ph.i * QUADS + (g + 1) * T)
                dve.reciprocal(rden1[:], DEN[:]).then_inc(back_step, 1)
                dve.wait_ge(back_step, ph.i * BACK_STEPS + g + 1)
                dve.tensor_tensor(OT[:, g, :], PV[:], rden1[:], ALU.mult).then_inc(normalised, 1)

            def add_residual(ph):
                dve.wait_ge(res_ready, ph.i + 1)
                for n, bank in enumerate((PV, DEN)):
                    dve.wait_ge(proj_filled, ph.i * 2 + n + 1)
                    dve.tensor_tensor(z[:, 2 * n:2 * n + 2, :], bank[:].rearrange("p (t e) -> p t e", t=2),
                                      res[:, 2 * n:2 * n + 2, :], ALU.add).then_inc(z_added, 1)

            def norm1(ph):
                base = ph.i * BACK_STEPS + GROUPS
                dve.wait_ge(z_added, ph.i * 2 + 2)
                for t in range(T):
                    dve.bn_stats(st1[:, t, :], z[:, t, :]).then_inc(back_step, 1)
                dve.wait_ge(back_step, base + T)
                dve.memset(scratch[:], 0.0)
                for t in range(T):
                    dve.bn_aggr(mv1[:, t, :], st1[:, t, :]).then_inc(stats1_ready, 1)
                dve.wait_ge(rstd1_ready, ph.i + 1)
                for t in range(T):
                    dve.tensor_scalar(zn[:, t, :], z[:, t, :], mv1[:, t, 0:1], rstd1[:, t:t + 1],
                                      ALU.subtract, ALU.mult).then_inc(zn_ready, 1)

            def step(ph):
                f, b = ph.front, ph.back
                if b:
                    clip(ph)
                if f:
                    lo(ph, "q0_0", Q0L, Q0H, 0, BQ0, 0)
                    lo(ph, "q0_1", Q0L, Q0H, 1, BQ0, 1)
                    lo(ph, "k0_0", K0L, K0H, 0, BK0, 2)
                    lo(ph, "k0_1", K0L, K0H, 1, BK0, 3)
                if b:
                    max1(ph, 1, 0, 8)
                if f:
                    bias(ph)
                    max0(ph, 0)
                    max0(ph, 1)
                if b:
                    max1(ph, 1, 8, 12)
                if f:
                    max0(ph, 2)
                    max0(ph, 3)
                if b:
                    max1(ph, 1, 12, 16)
                    mrow1(ph, 1)
                if f:
                    mrow0(ph)
                if b:
                    normalise(ph, 0)
                if f:
                    for t in range(T):
                        context0(ph, t)
                    norm0(ph)
                    lo(ph, "q1_0", Q1L, Q1H, 0, BQ1, 4)
                    lo(ph, "k1_0", K1L, K1H, 0, BK1, 5)
                    max1(ph, 0, 0, 8)
                    lo(ph, "q1_1", Q1L, Q1H, 1, BQ1, 6)
                    lo(ph, "k1_1", K1L, K1H, 1, BK1, 7)
                if b:
                    normalise(ph, 1)
                if f:
                    max1(ph, 0, 8, 14)
                if b:
                    add_residual(ph)
                if f:
                    max1(ph, 0, 14, 16)
                    mrow1(ph, 0)
                if b:
                    norm1(ph)

            run(dve, step)

        @block.gpsimd
        def _(pool):
            POOL_STEPS0 = 1
            POOL_STEPS1 = 3

            pool.memset(og[:, 0, 0:1], 0.0).then_inc(out_stored, 1)
            pool.memset(ident[:], 0.0).then_inc(ident_zeroed, 1)
            pool.wait_ge(ident_zeroed, 1)
            pool.affine_select(out=ident[:], in_=ident[:], compare_op=ALU.not_equal, fill=1.0, base=0,
                               pattern=[[-1, P]], channel_multiplier=1).then_inc(ident_ready, 1)
            pool.wait_ge(consts_set, 7)
            pool.wait_ge(spread_ready, 4)

            def all_rows(n):
                return spread[:, n, :].unsqueeze(1).broadcast_to([P, T, D])

            def residual(ph):
                pool.wait_ge(xn_ready, ph.i * T + T)
                pool.tensor_tensor(res[:], xn[:], all_rows(S_G0), ALU.mult).then_inc(pool_step1, 1)
                pool.wait_ge(pool_step1, ph.i * POOL_STEPS1 + 1)
                pool.tensor_tensor(res[:], res[:], all_rows(S_RES), ALU.add).then_inc(res_ready, 1)

            def rstd(var, ve, dst, step_sem, before, done):
                pool.tensor_tensor(ve[:], var, eps[:], ALU.add).then_inc(step_sem, 1)
                pool.wait_ge(step_sem, before + 1)
                pool.tensor_tensor(dst[:], ve[:], minus_half[:], ALU.pow).then_inc(done, 1)

            def mask(ph, quad):
                k = quad % T
                for pair in range(2):
                    if quad == 0 and pair == 0:
                        pool.wait_ge(adj_clipped, ph.i + 1)
                    pool.wait_ge(exp_done, ph.i * UNITS + 2 * quad + pair + 1)
                    w = PR[quad % 2][:, 2 * pair:2 * pair + 2, :]
                    pool.tensor_tensor(w, w, CLIP[:, k, :].unsqueeze(1).broadcast_to([P, 2, N]),
                                       ALU.mult).then_inc(masked, 1)

            def rstd0_of(ph):
                pool.wait_ge(stats0_ready, ph.j * T + T)
                rstd(mv0[:, :, 1], ve0, rstd0, pool_step0, ph.j * POOL_STEPS0, rstd0_ready)

            def output(ph):
                pool.wait_ge(zn_ready, ph.i * T + T)
                pool.wait_ge(out_stored, ph.i * DMA + 1)
                pool.tensor_tensor(og[:], zn[:], all_rows(S_G1), ALU.mult).then_inc(pool_step1, 1)
                pool.wait_ge(pool_step1, ph.i * POOL_STEPS1 + 3)
                pool.tensor_tensor(og[:], og[:], all_rows(S_B1), ALU.add).then_inc(out_ready, 1)

            def step(ph):
                f, b = ph.front, ph.back
                if b:
                    residual(ph)
                    for quad in range(5):
                        mask(ph, quad)
                if f:
                    rstd0_of(ph)
                if b:
                    for quad in range(5, QUADS):
                        mask(ph, quad)
                    pool.wait_ge(stats1_ready, ph.i * T + T)
                    rstd(mv1[:, :, 1], ve1, rstd1, pool_step1, ph.i * POOL_STEPS1 + 1, rstd1_ready)
                    output(ph)

            run(pool, step)


def kernel(**inputs):
    import numpy as np
    import concourse.bacc as bacc
    from concourse.bass_utils import run_bass_kernel_spmd

    nc = bacc.Bacc("TRN2", target_bir_lowering=False, num_devices=1)
    arrays, args = {}, []

    def give(name, a):
        a = np.ascontiguousarray(a)
        arrays[name] = a
        args.append(nc.dram_tensor(name, a.shape, mybir.dt.from_np(a.dtype), kind="ExternalInput").ap())

    x, adj = np.asarray(inputs["x"]), np.asarray(inputs["adj"])
    give("x", x)
    give("x_t", x.transpose(0, 2, 1))
    give("adj_t", adj.transpose(0, 2, 1))
    for name in ("L0_gnn_Wq", "L0_gnn_Wk", "L0_gnn_Wc"):
        give(name, np.asarray(inputs[name]))
    for name in ("L1_gnn_Wq", "L1_gnn_Wk", "L1_gnn_Wv", "L1_gnn_Wo"):
        give(name, np.asarray(inputs[name]).T)
    cols = np.stack([np.asarray(inputs[name]) for name in COLS])
    give("channel_cols", cols.reshape(len(COLS), -1, P).transpose(2, 0, 1))
    give("channel_rows", np.stack([np.asarray(inputs[name]) for name in ROWS])[None])
    args.append(nc.dram_tensor("out", x.shape, mybir.dt.from_np(x.dtype), kind="ExternalOutput").ap())
    two_layer_graph_attention(nc, *args)
    r = run_bass_kernel_spmd(nc, [arrays], core_ids=[0])
    return r.results[0]["out"]
```

```python
from contextlib import ExitStack

import concourse.bass as bass
from concourse import mybir

F32 = mybir.dt.float32
F32R = mybir.dt.float32r
BF16 = mybir.dt.bfloat16
ALU = mybir.AluOpType
ACT = mybir.ActivationFunctionType
AX = mybir.AxisListType

P = 128
HEADS = 8
PER_GROUP = 4
GROUPS = HEADS // PER_GROUP
MASKED = -1e18
MAX_FLOOR = -1e17
ADJ_MIN = 1e-8
WEIGHT_BUFFERS = 3
LN_EPS = 1e-5
TINY = 1e-30
DMA = 16


class Phase:

    def __init__(self, t, i, j):
        self.t, self.i, self.j = t, i, j
        self.tail, self.back, self.front = (n is not None for n in (t, i, j))
        self.kind = ("steady" if self.front else "last") if self.back else ("first" if self.front else "end")


def maxima(group, *range_):
    return [("max1", group, n) for n in range(*range_)]


SCHEDULE = (
    [("split", 0), ("split", 1)] + maxima(1, 0, 3) + [("q0", 0), ("reciprocal", 1, 0), ("reciprocal", 1, 1)]
    + [("q0", 1), ("scores1", 0, 0), ("reciprocal", 1, 2), ("k0", 0), ("scores1", 0, 1)]
    + [("bias",), ("k0", 1), ("scores1", 1, 0), ("reciprocal", 1, 3), ("normalise", 1), ("u", 0)] + maxima(1, 3, 4)
    + [("scores1", 1, 1), ("max0", 0), ("max0", 1), ("project",), ("max0", 2), ("max0", 3), ("u", 1), ("mrow0",), ("stats1",)]
    + [("values1", 0), ("denominators1", 0)]
    + maxima(1, 4, 6) + [("scores0", 0), ("norm1",), ("scores1", 2, 0)] + maxima(1, 6, 8) + [("scores0", 1)]
    + [("scores1", 2, 1), ("output",), ("values1", 1)]
    + maxima(1, 8, 10) + [("scores0", 2), ("scores1", 3, 0)] + maxima(1, 10, 12) + [("denominators1", 1)]
    + [("scores1", 3, 1), ("scores0", 3), ("skip_back",)] + maxima(1, 12, 14) + [("residual",), ("values1", 2)]
    + maxima(1, 14, 16) + [("context0", 0), ("skip_back",), ("denominators1", 2), ("mrow1", 1)]
    + [("context0", 1), ("values1", 3), ("scores1", 4, 0), ("mask", 4, 0), ("context0", 2)]
    + [("scores1", 4, 1), ("denominators1", 3), ("sums_out", 0), ("context0", 3), ("skip_back",), ("scores1", 5, 0)]
    + [("values1", 4), ("stats0",), ("mask", 5, 0), ("norm0",), ("scores1", 5, 1), ("denominators1", 4), ("scores1", 6, 0)]
    + [("transpose", 0), ("transpose", 1), ("reciprocal", 0, 0), ("reciprocal", 0, 1), ("reciprocal", 0, 2), ("reciprocal", 0, 3)]
    + [("values1", 5), ("scores1", 6, 1), ("denominators1", 5), ("q1", 0), ("normalise", 0), ("k1", 0)]
    + [("scores1", 7, 0), ("values1", 6)] + maxima(0, 0, 3) + [("q1", 1)] + maxima(0, 3, 6)
    + [("scores1", 7, 1), ("denominators1", 6)] + maxima(0, 6, 9) + [("k1", 1)] + maxima(0, 9, 12)
    + [("values1", 7), ("clip",)] + maxima(0, 12, 14) + [("denominators1", 7), ("sums_out", 1), ("v", 0)]
    + maxima(0, 14, 16) + [("v", 1), ("mrow1", 0)]
)

DVE_MASKS = [s[1:] for s in SCHEDULE if s[0] == "mask"]


def masks(by_dve, quad):
    n = sum(1 for q, _ in DVE_MASKS if q <= quad)
    return n if by_dve else 2 * quad + 2 - n


MISC_BANKS = 4
MISC_DRAIN = {
    "q0": "dve", "k0": "dve", "u": "act", "max0": "dve", "mrow0": "dve", "scores0": "act",
    "context0": "dve", "transpose": "dve", "q1": "dve", "k1": "dve", "v": "act", "max1": "dve",
    "mrow1": "dve",
    "skip_back": None,
}
BACK = ("residual", "mask", "scores1", "values1", "denominators1", "sums_out",
        "reciprocal", "normalise", "skip_back")
TAIL = ("project", "stats1", "norm1", "output")
SPLIT = ("q0", "k0", "transpose", "q1", "k1")


def is_back(stage):
    return stage[0] in BACK or stage[:2] in (("max1", 1), ("mrow1", 1))


def is_tail(stage):
    return stage[0] in TAIL or stage[:2] in (("reciprocal", GROUPS - 1), ("normalise", GROUPS - 1))


def stages(ph):
    return [s for s in SCHEDULE if (ph.tail if is_tail(s) else ph.back if is_back(s) else ph.front)]


class MiscBanks:

    def __init__(self, graphs):
        self.uses = {ph.kind: [s for s in stages(ph) if s[0] in MISC_DRAIN]
                     for ph in (Phase(None, None, 0), Phase(0, 1, 2), Phase(0, 1, None))}
        assert all(len(self.uses[k]) % MISC_BANKS == 0 for k in ("first", "steady"))
        self.graphs = graphs

    @staticmethod
    def _number(uses, what):
        return sum(1 for s in uses if MISC_DRAIN[s[0]] and what in ("fill", MISC_DRAIN[s[0]]))

    def _base(self, ph, what):
        first, steady = (self._number(self.uses[k], what) for k in ("first", "steady"))
        if ph.kind == "first":
            return 0
        return (ph.i if ph.kind == "steady" else self.graphs - 1) * steady + first

    def bank(self, ph, *stage):
        return self.uses[ph.kind].index(stage) % MISC_BANKS

    def count(self, ph, what, *stage):
        uses = self.uses[ph.kind]
        return self._base(ph, what) + self._number(uses[: uses.index(stage) + 1], what)

    def count_before(self, ph, *stage):
        uses, e = self.uses["steady"], MISC_DRAIN[stage[0]]
        later = [s for s in uses[uses.index(stage) + 1:] if MISC_DRAIN[s[0]] == e]
        assert not any(map(is_back, later))
        return self._base(ph, e) - self._number(later, e)

    def before(self, ph, *stage):
        uses = self.uses[ph.kind]
        n = uses.index(stage) - MISC_BANKS
        while n >= 0 and MISC_DRAIN[uses[n][0]] is None:
            n -= MISC_BANKS
        if n >= 0:
            e = MISC_DRAIN[uses[n][0]]
            return e, self.count(ph, e, *uses[n])
        if ph.kind == "first":
            return None
        use = self.uses["steady"][n]
        e = MISC_DRAIN[use[0]]
        return e, self.count_before(ph, *use)


COLS = ("L0_gnn_bq", "L0_gnn_bk", "L1_gnn_bq", "L1_gnn_bk", "L1_gnn_bv", "L0_gnn_gamma", "L0_gnn_beta")
ROWS = ("L0_gnn_gamma", "L0_gnn_beta", "L1_gnn_bo", "L1_gnn_gamma", "L1_gnn_beta")


def two_layer_graph_attention(nc, x, x_t, adj_t, wq0, wk0, wc0, wq1_t, wk1_t, wv1_t, wo1_t,
                              channel_cols, channel_rows, out):
    B, N, D = x.shape
    T = N // P
    C = D // P
    DK = D // HEADS
    SCALE0 = float(D) ** -0.5
    SCALE1 = float(DK) ** -0.5
    assert (T, C, DK, GROUPS) == (4, 2, 32, C) and HEADS * DK == D
    HI_HI, HI_LO, LO_HI, MROW = 0, DK, 2 * DK, 3 * DK
    STACK = 3 * DK + 1
    MAXIMA = PER_GROUP * T
    TILES = HEADS * T
    PAIRS = TILES // 2
    QUADS = GROUPS * T
    STACK_DMAS = 6 * PER_GROUP

    misc = MiscBanks(B)

    with ExitStack() as ctx:
        def sb(name, shape, dt=F32):
            return ctx.enter_context(nc.sbuf_tensor(name, shape, dt))

        def ps(name, shape):
            return ctx.enter_context(nc.psum_tensor(name, shape, F32))

        def sem(name):
            return ctx.enter_context(nc.semaphore(name))

        ident = sb("ident", [P, P])
        ident_bf = sb("ident_bf", [P, P], BF16)
        ones = sb("ones", [P, P])
        ones_r = sb("ones_r", [1, P], F32R)
        minus_half = sb("minus_half", [P, T])
        eps = sb("eps", [P, T])
        scratch = sb("scratch", [P, 1])
        split_weights = [tuple(sb(n + part, [P, C, D], F32R) for part in ("_high", "_low"))
                         for n in ("Wq0", "Wk0", "Wc0", "Wq1", "Wk1", "Wv1")]
        Wq0, Wk0, Wc0, Wq1, Wk1, Wv1 = split_weights
        Wo1 = sb("Wo1", [P, C, D])
        cols = sb("cols", [P, len(COLS), C])
        BQ0, BK0, BQ1, BK1, BV1, G0, B0 = range(len(COLS))
        R_G0, R_B0, R_BO, R_G1, R_B1 = range(len(ROWS))
        spread = sb("spread", [P, 4, D])
        S_G0, S_RES, S_G1, S_B1 = range(4)

        X = sb("X", [P, T, D])
        XTH, XTL = (sb(n, [P, C, N], F32R) for n in ("XTH", "XTL"))
        ADJ = sb("ADJ", [P, T, N])
        BIAS = sb("BIAS", [P, T, N], BF16)
        Q0H, Q0L, K0H, K0L = (sb(n, [P, C, N], F32R) for n in ("Q0H", "Q0L", "K0H", "K0L"))
        U = sb("U", [P, T, D + 1])
        mx0 = sb("mx0", [P, T])
        nm0 = sb("nm0", [1, N], F32R)
        P0 = sb("P0", [P, T, N])
        XT = P0[:, 0:C, :]
        den0 = sb("den0", [P, T])
        rden0 = sb("rden0", [P, T])
        st0 = sb("st0", [P, T, 6])
        mv0 = sb("mv0", [P, T, 2])
        ve0 = sb("ve0", [P, T])
        rstd0 = sb("rstd0", [P, T])
        xn = sb("xn", [P, T, D])
        XNH, XNL = (sb(n, [P, C, N], F32R) for n in ("XNH", "XNL"))
        Q1H, Q1L, K1H, K1L = (sb(n, [P, C, N], F32R) for n in ("Q1H", "Q1L", "K1H", "K1L"))
        mx1 = sb("mx1", [P, GROUPS, PER_GROUP, T])
        nm1 = [sb(f"nm1_{g}", [MAXIMA, P], F32R) for g in range(GROUPS)]
        QS = sb("QS", [STACK, HEADS, N], F32R)
        KS = sb("KS", [STACK, HEADS, N], F32R)

        V = sb("V", [P, T, D])
        CLIP = sb("CLIP", [P, T, N])
        PR = [sb(f"PR{n}", [P, PER_GROUP, N]) for n in range(WEIGHT_BUFFERS)]
        sums_v = sb("sums_v", [P, N])
        sums_w = sb("sums_w", [P, N])
        raw_weights = [PR[n // PER_GROUP][:, n % PER_GROUP, :].rearrange("p (c e) -> p c e", c=C)
                       for n in range(len(split_weights))]
        flat = PR[2][:].rearrange("p t n -> p (t n)")
        rows = flat[0:1, 0:len(ROWS) * D].rearrange("p (v e) -> p v e", e=D)
        bv_wide = flat[:, len(ROWS) * D:len(ROWS) * D + C * P].rearrange("p (c q) -> p c q", q=P)
        rden1 = sb("rden1", [P, N])
        OT = sb("OT", [P, C, N])
        res = sb("res", [P, T, D])
        z = sb("z", [P, T, D])
        st1 = sb("st1", [P, T, 6])
        mv1 = sb("mv1", [P, T, 2])
        ve1 = sb("ve1", [P, T])
        rstd1 = sb("rstd1", [P, T])

        MISC = [ps(f"misc{n}", [P, N]) for n in range(MISC_BANKS)]
        ST = [ps(f"scores{n}", [P, N]) for n in range(2)]
        PV = ps("values", [P, N])
        DEN = ps("denominators", [P, N])

        weights_loaded = sem("weights_loaded")
        consts_set = sem("consts_set")
        ident_zeroed = sem("ident_zeroed")
        ident_ready = sem("ident_ready")
        bv_widened = sem("bv_widened")
        spread_filled = sem("spread_filled")
        spread_ready = sem("spread_ready")
        bias_columns_filled = sem("bias_columns_filled")
        bias_columns_added = sem("bias_columns_added")
        weight_scaled = sem("weight_scaled")
        weight_high = sem("weight_high")
        weight_low = sem("weight_low")
        x_loaded = sem("x_loaded")
        xt_loaded = sem("xt_loaded")
        xt_high = sem("xt_high")
        xt_low = sem("xt_low")
        adj_loaded = sem("adj_loaded")
        misc_filled = sem("misc_filled")
        misc_drained = {"act": sem("misc_drained_act"), "dve": sem("misc_drained_dve")}
        hi_written = sem("hi_written")
        bias_built = sem("bias_built")
        adj_clipped = sem("adj_clipped")
        front_step = sem("front_step")
        stats_step = sem("stats_step")
        back_step = sem("back_step")
        tail_step = sem("tail_step")
        stats0_ready = sem("stats0_ready")
        rstd0_ready = sem("rstd0_ready")
        xn_ready = sem("xn_ready")
        pool_step0 = sem("pool_step0")
        res_step = sem("res_step")
        pool_step1 = sem("pool_step1")
        stack_loaded = [sem(f"stack_loaded{g}") for g in range(GROUPS)]
        mrow_loaded = [sem(f"mrow_loaded{g}") for g in range(GROUPS)]
        scores_filled = sem("scores_filled")
        exp_done = sem("exp_done")
        masked_pool = sem("masked_pool")
        masked_dve = sem("masked_dve")
        quad_summed = sem("quad_summed")
        sums_out = sem("sums_out")
        normalised = sem("normalised")
        proj_filled = sem("proj_filled")
        z_added = sem("z_added")
        stats1_ready = sem("stats1_ready")
        rstd1_ready = sem("rstd1_ready")
        zn_ready = sem("zn_ready")
        res_ready = sem("res_ready")
        out_ready = sem("out_ready")
        out_stored = sem("out_stored")

        LOADS = 7 + 2
        CONSTS = 7
        block = ctx.enter_context(nc.Block())

        def misc_bank(ph, *stage):
            return MISC[misc.bank(ph, *stage)]

        def wait_drained(eng, ph, *stage):
            e = MISC_DRAIN[stage[0]]
            eng.wait_ge(misc_drained[e], misc.count(ph, e, *stage))

        def wait_filled(eng, ph, *stage):
            eng.wait_ge(misc_filled, misc.count(ph, "fill", *stage))

        def mask_operands(quad, pair):
            w = PR[quad % WEIGHT_BUFFERS][:, 2 * pair:2 * pair + 2, :]
            return w, CLIP[:, quad % T, :].unsqueeze(1).broadcast_to([P, 2, N])

        def run(eng, step):
            step(Phase(None, None, 0))
            step(Phase(None, 0, 1))
            with eng.Fori(1, B - 1) as i:
                step(Phase(i - 1, i, i + 1))
            step(Phase(B - 2, B - 1, None))
            step(Phase(B - 1, None, None))

        def follow(ph, do):
            for stage, *where in stages(ph):
                if stage in do:
                    do[stage](ph, *where)

        @block.sync
        def _(sp):
            for w, src in zip(raw_weights + [Wo1[:]], (wq0, wk0, wc0, wq1_t, wk1_t, wv1_t, wo1_t)):
                sp.dma_start(w, src.rearrange("(c p) e -> p c e", p=P)).then_inc(weights_loaded, DMA)
            sp.dma_start(cols[:], channel_cols).then_inc(weights_loaded, DMA)
            sp.dma_start(rows, channel_rows).then_inc(weights_loaded, DMA)

            def load_stacks(g):
                for h in range(PER_GROUP):
                    part = slice(DK * h, DK * (h + 1))
                    for stack, parts in ((QS, (Q1H, Q1H, Q1L)), (KS, (K1H, K1L, K1H))):
                        for row, src in zip((HI_HI, HI_LO, LO_HI), parts):
                            sp.dma_start(stack[row:row + DK, PER_GROUP * g + h, :].bitcast(F32),
                                         src[part, g, :].bitcast(F32)).then_inc(stack_loaded[g], DMA)

            def load_mrow(g):
                row = QS[MROW:STACK, PER_GROUP * g:PER_GROUP * (g + 1), :].bitcast(F32)
                sp.dma_start(row.rearrange("o h (t q) -> o (h t) q", q=P),
                             nm1[g][:].bitcast(F32)).then_inc(mrow_loaded[g], DMA)

            def load_xt(j):
                sp.dma_start(XT, x_t[j].rearrange("(c p) n -> p c n", p=P)).then_inc(xt_loaded, DMA)

            def load_x(j):
                sp.dma_start(X[:], x[j].rearrange("(t p) e -> p t e", p=P)).then_inc(x_loaded, DMA)

            def load_adj(j):
                sp.dma_start(ADJ[:], adj_t[j].rearrange("(t p) q -> p t q", p=P)).then_inc(adj_loaded, DMA)

            def load_second_mrow(ph):
                wait_drained(sp, ph, "mrow1", 1)
                load_mrow(1)

            def store(i):
                sp.wait_ge(out_ready, i + 1)
                sp.dma_start(out[i].rearrange("(t p) e -> p t e", p=P), z[:]).then_inc(out_stored, DMA)

            def finish_front(ph):
                i, j = ph.i, ph.j
                sp.wait_ge(misc_drained["dve"], misc.count_before(ph, "k1", 0))
                if ph.front:
                    load_xt(j)
                load_stacks(0)
                sp.wait_ge(misc_drained["dve"], misc.count_before(ph, "mrow1", 0))
                load_mrow(0)
                if ph.front:
                    sp.wait_ge(adj_clipped, i + 1)
                    load_adj(j)
                load_stacks(1)
                if ph.front:
                    load_x(j)

            load_xt(0)
            load_adj(0)
            load_x(0)
            first = Phase(None, 0, 1)
            finish_front(first)
            load_second_mrow(first)
            with sp.Fori(1, B - 1) as i:
                ph = Phase(i - 1, i, i + 1)
                finish_front(ph)
                store(i - 1)
                load_second_mrow(ph)
            last = Phase(B - 2, B - 1, None)
            finish_front(last)
            store(B - 2)
            load_second_mrow(last)
            store(B - 1)
            sp.wait_ge(out_stored, B * DMA + 1)

        @block.tensor
        def _(pe):
            def fill(ph, *stage):
                before = misc.before(ph, *stage)
                if before is not None:
                    pe.wait_ge(misc_drained[before[0]], before[1])
                return misc_bank(ph, *stage)

            pe.wait_ge(weights_loaded, LOADS * DMA)
            pe.wait_ge(consts_set, CONSTS)
            pe.wait_ge(ident_ready, 2)
            for n, w in enumerate(raw_weights[3:]):
                for c in range(C):
                    for k in range(C):
                        mm = pe.matmul(ST[0][:, C * n + c:C * n + c + 1],
                                       w[:, k, P * c:P * (c + 1)], cols[:, B0, k:k + 1],
                                       start=(k == 0), stop=(k == C - 1))
            mm.then_inc(bias_columns_filled, 1)
            pe.wait_ge(bv_widened, C)
            one = ones[0:1, :]
            pe.matmul(MISC[0][:, 0:D], one, rows[:, R_G0, :], start=True, stop=True)
            for n in (R_B0, R_BO):
                pe.matmul(MISC[1][:, 0:D], one, rows[:, n, :], start=(n == R_B0), stop=False)
            for c in range(C):
                pe.matmul(MISC[1][:, 0:D], bv_wide[:, c, :], Wo1[:, c, :], start=False, stop=(c == C - 1))
            pe.matmul(MISC[2][:, 0:D], one, rows[:, R_G1, :], start=True, stop=True)
            pe.matmul(MISC[3][:, 0:D], one, rows[:, R_B1, :], start=True, stop=True).then_inc(spread_filled, 1)
            pe.wait_ge(spread_ready, 4)

            def products(weights, src):
                return [(w, s, k) for w, s in ((weights[0], src[0]), (weights[1], src[0]), (weights[0], src[1]))
                        for k in range(C)]

            def project(ph, stage, c, weights, src, wait_for=None):
                bank = fill(ph, stage, c)
                terms = products(weights, src)
                for n, (w, s, k) in enumerate(terms):
                    if wait_for:
                        wait_for(s, k)
                    mm = pe.matmul(bank[:], w[:, k, P * c:P * (c + 1)], s[:, k, :],
                                   start=(n == 0), stop=(n == len(terms) - 1))
                mm.then_inc(misc_filled, 1)

            def project_rows(ph, stage, m, weights, src):
                bank = fill(ph, stage, m)
                terms = products(weights, src)
                for half in range(2):
                    t = 2 * m + half
                    for n, (w, s, k) in enumerate(terms):
                        mm = pe.matmul(bank[:, D * half:D * (half + 1)], s[:, k, P * t:P * (t + 1)],
                                       w[:, k, :], start=(n == 0), stop=(n == len(terms) - 1))
                mm.then_inc(misc_filled, 1)

            X_PARTS, XN_PARTS = (XTH, XTL), (XNH, XNL)
            pe.wait_ge(weight_low, len(split_weights))

            def q0(ph, c):
                def wait_for_x(part, k):
                    pe.wait_ge(xt_high if part is XTH else xt_low, ph.j * C + k + 1)

                project(ph, "q0", c, Wq0, X_PARTS, wait_for_x if c == 0 else None)

            def q1(ph, c):
                if c == 0:
                    wait_drained(pe, ph, "transpose", 1)
                project(ph, "q1", c, Wq1, XN_PARTS)

            def max0(ph, t):
                if t == 0:
                    wait_drained(pe, ph, "k0", 1)
                    pe.wait_ge(bias_built, ph.j + 1)
                bank = fill(ph, "max0", t)
                q = slice(P * t, P * (t + 1))
                for c in range(C):
                    pe.matmul(bank[:], Q0H[:, c, q], K0H[:, c, :], start=(c == 0), stop=False)
                for k in range(T):
                    mm = pe.matmul(bank[:, P * k:P * (k + 1)], BIAS[:, k, q], ident_bf[:],
                                   start=False, stop=(k == T - 1))
                mm.then_inc(misc_filled, 1)

            def mrow0(ph):
                wait_drained(pe, ph, "max0", T - 1)
                bank = fill(ph, "mrow0")
                for t in range(T):
                    mm = pe.matmul(bank[0:1, P * t:P * (t + 1)], mx0[:, t:t + 1], ident[:],
                                   start=True, stop=True)
                mm.then_inc(misc_filled, 1)

            def scores0(ph, k):
                if k == 0:
                    wait_drained(pe, ph, "mrow0")
                bank = fill(ph, "scores0", k)
                rows_k = slice(P * k, P * (k + 1))
                n = 0
                for c in range(C):
                    for kk, qq in ((K0H, Q0H), (K0L, Q0H), (K0H, Q0L)):
                        pe.matmul(bank[:], kk[:, c, rows_k], qq[:, c, :], start=(n == 0), stop=False)
                        n += 1
                pe.matmul(bank[:], ones_r[:], nm0[:], start=False, stop=False)
                pe.matmul(bank[:], ident_bf[:], BIAS[:, k, :], start=False, stop=True).then_inc(misc_filled, 1)

            def context0(ph, t):
                if t == 0:
                    wait_drained(pe, ph, "scores0", T - 1)
                bank = fill(ph, "context0", t)
                for k in range(T):
                    mm = pe.matmul(bank[:, 0:D + 1], P0[:, k, P * t:P * (t + 1)], U[:, k, :],
                                   start=(k == 0), stop=(k == T - 1))
                mm.then_inc(misc_filled, 1)

            def transpose(ph, c):
                bank = fill(ph, "transpose", c)
                for t in range(T):
                    if c == 0:
                        pe.wait_ge(xn_ready, ph.j * T + t + 1)
                    mm = pe.transpose(bank[:, P * t:P * (t + 1)], xn[:, t, P * c:P * (c + 1)], ident[:])
                mm.then_inc(misc_filled, 1)

            def max1(ph, g, n):
                if n == 0 and g == 0:
                    wait_drained(pe, ph, "k1", 0)
                elif n == 0:
                    pe.wait_ge(misc_drained["dve"], misc.count_before(ph, "k1", 1))
                bank = fill(ph, "max1", g, n)
                t, h = divmod(n, PER_GROUP)
                part = slice(DK * h, DK * (h + 1))
                pe.matmul(bank[:], Q1H[part, g, P * t:P * (t + 1)], K1H[part, g, :],
                          start=True, stop=True).then_inc(misc_filled, 1)

            def mrow1(ph, g):
                wait_drained(pe, ph, "max1", g, PER_GROUP * T - 1)
                pe.matmul(fill(ph, "mrow1", g)[0:MAXIMA, 0:P], mx1[:, g, :, :].rearrange("p h t -> p (h t)"),
                          ident[:], start=True, stop=True).then_inc(misc_filled, 1)

            def scores1(ph, quad, pair):
                g, k = divmod(quad, T)
                if k == 0 and pair == 0:
                    pe.wait_ge(stack_loaded[g], (ph.i + 1) * (STACK_DMAS * DMA))
                    pe.wait_ge(mrow_loaded[g], (ph.i + 1) * DMA)
                for n in range(2):
                    tile = PER_GROUP * quad + 2 * pair + n
                    if tile >= 2:
                        pe.wait_ge(exp_done, ph.i * TILES + tile - 1)
                    h = PER_GROUP * g + 2 * pair + n
                    pe.matmul(ST[n][:], KS[:, h, P * k:P * (k + 1)], QS[:, h, :],
                              start=True, stop=True).then_inc(scores_filled, 1)

            def sums1(ph, quad, bank, first):
                g, k = divmod(quad, T)
                if first:
                    pe.wait_ge(masked_pool, ph.i * masks(False, QUADS - 1) + masks(False, quad))
                    if any(q == quad for q, _ in DVE_MASKS):
                        pe.wait_ge(masked_dve, ph.i * len(DVE_MASKS) + masks(True, quad))
                    if quad == 0:
                        pe.wait_ge(misc_drained["act"], misc.count_before(ph, "v", 1))
                        pe.wait_ge(z_added, ph.i * 2 + 1)
                    elif k == 0:
                        pe.wait_ge(sums_out, (ph.i * GROUPS + g) * 2)
                for h in range(PER_GROUP):
                    c = DK * (PER_GROUP * g + h)
                    w = V[:, k, c:c + DK] if bank is PV else ones[:, 0:DK]
                    mm = pe.matmul(bank[DK * h:DK * (h + 1), :], w, PR[quad % WEIGHT_BUFFERS][:, h, :],
                                   start=(k == 0), stop=(k == T - 1))
                return mm

            def values_first(quad):
                return SCHEDULE.index(("values1", quad)) < SCHEDULE.index(("denominators1", quad))

            def values1(ph, quad):
                first = values_first(quad)
                mm = sums1(ph, quad, PV, first)
                if not first:
                    mm.then_inc(quad_summed, 1)

            def denominators1(ph, quad):
                first = not values_first(quad)
                mm = sums1(ph, quad, DEN, first)
                if not first:
                    mm.then_inc(quad_summed, 1)

            def project_out(ph):
                pe.wait_ge(normalised, ph.t * GROUPS + GROUPS)
                for t in range(T):
                    bank = (PV, DEN)[t // 2]
                    for c in range(C):
                        mm = pe.matmul(bank[:, D * (t % 2):D * (t % 2 + 1)], OT[:, c, P * t:P * (t + 1)],
                                       Wo1[:, c, :], start=(c == 0), stop=(c == C - 1))
                    if t % 2:
                        mm.then_inc(proj_filled, 1)

            do = {
                "q0": q0,
                "k0": lambda ph, c: project(ph, "k0", c, Wk0, X_PARTS),
                "u": lambda ph, n: project_rows(ph, "u", n, Wc0, X_PARTS),
                "max0": max0, "mrow0": mrow0, "scores0": scores0, "context0": context0,
                "transpose": transpose, "q1": q1,
                "k1": lambda ph, c: project(ph, "k1", c, Wk1, XN_PARTS),
                "v": lambda ph, n: project_rows(ph, "v", n, Wv1, XN_PARTS),
                "max1": max1, "mrow1": mrow1, "scores1": scores1, "values1": values1,
                "denominators1": denominators1, "project": project_out,
            }
            run(pe, lambda ph: follow(ph, do))

        @block.scalar
        def _(act):
            act.wait_ge(weights_loaded, LOADS * DMA)
            act.wait_ge(spread_filled, 1)
            for n in range(4):
                act.copy(spread[:, n, :], MISC[n][:, 0:D]).then_inc(spread_ready, 1)

            for n, ((high, _), raw) in enumerate(zip(split_weights, raw_weights)):
                if n >= 3:
                    act.wait_ge(weight_scaled, (n - 2) * C)
                act.copy(high[:], raw).then_inc(weight_high, 1)

            def split(ph, c):
                if c == 0:
                    act.wait_ge(xt_loaded, ph.j * DMA + DMA)
                act.copy(XTH[:, c, :], XT[:, c, :]).then_inc(xt_high, 1)

            def hi(ph, stage, c, dst, bias):
                wait_filled(act, ph, stage, c)
                act.activation(dst[:, c, :], misc_bank(ph, stage, c)[:], ACT.Identity,
                               bias=cols[:, bias, c:c + 1]).then_inc(hi_written, 1)

            def rows_out(ph, stage, n, dst):
                wait_filled(act, ph, stage, n)
                act.copy(dst[:, 2 * n:2 * n + 2, 0:D],
                         misc_bank(ph, stage, n)[:].rearrange("p (t e) -> p t e", t=2))\
                   .then_inc(misc_drained["act"], 1)

            def exp0(ph, k):
                wait_filled(act, ph, "scores0", k)
                act.activation(P0[:, k, :], misc_bank(ph, "scores0", k)[:], ACT.Exp,
                               scale=SCALE0).then_inc(misc_drained["act"], 1)

            def exp1(ph, quad, pair):
                if quad >= WEIGHT_BUFFERS and pair == 0:
                    act.wait_ge(quad_summed, ph.i * QUADS + quad - WEIGHT_BUFFERS + 1)
                for n in range(2):
                    h = 2 * pair + n
                    act.wait_ge(scores_filled, ph.i * TILES + PER_GROUP * quad + h + 1)
                    act.activation(PR[quad % WEIGHT_BUFFERS][:, h, :], ST[n][:], ACT.Exp,
                                   scale=SCALE1).then_inc(exp_done, 1)

            def copy_sums(ph, g):
                act.wait_ge(quad_summed, ph.i * QUADS + (g + 1) * T)
                if g > 0:
                    act.wait_ge(normalised, ph.i * GROUPS + g)
                act.copy(sums_w[:], DEN[:]).then_inc(sums_out, 1)
                act.copy(sums_v[:], PV[:]).then_inc(sums_out, 1)

            def xn_high(ph, c):
                wait_filled(act, ph, "transpose", c)
                act.copy(XNH[:, c, :], misc_bank(ph, "transpose", c)[:]).then_inc(hi_written, 1)

            do = {
                "split": split, "q0": lambda ph, c: hi(ph, "q0", c, Q0H, BQ0),
                "k0": lambda ph, c: hi(ph, "k0", c, K0H, BK0),
                "u": lambda ph, n: rows_out(ph, "u", n, U),
                "scores0": exp0, "transpose": xn_high,
                "q1": lambda ph, c: hi(ph, "q1", c, Q1H, BQ1),
                "k1": lambda ph, c: hi(ph, "k1", c, K1H, BK1),
                "v": lambda ph, n: rows_out(ph, "v", n, V),
                "scores1": exp1, "sums_out": copy_sums,
            }
            run(act, lambda ph: follow(ph, do))

        @block.vector
        def _(dve):
            FRONT_STEPS = 2 * T
            BACK_STEPS = GROUPS * T

            dve.memset(ones[:], 1.0).then_inc(consts_set, 1)
            dve.memset(ones_r[:].bitcast(F32), 1.0).then_inc(consts_set, 1)
            dve.memset(minus_half[:], -0.5).then_inc(consts_set, 1)
            dve.memset(eps[:], LN_EPS).then_inc(consts_set, 1)
            dve.memset(U[:, :, D:D + 1], 1.0).then_inc(consts_set, 1)
            dve.memset(KS[MROW:STACK, :, :].bitcast(F32), 1.0).then_inc(consts_set, 1)
            dve.memset(bv_wide, 0.0).then_inc(consts_set, 1)
            dve.memset(scratch[:], 0.0).then_inc(z_added, 1)
            dve.wait_ge(consts_set, CONSTS)
            dve.wait_ge(ident_ready, 1)
            dve.tensor_copy(ident_bf[:], ident[:]).then_inc(ident_ready, 1)
            dve.wait_ge(weights_loaded, LOADS * DMA)
            dve.wait_ge(bias_columns_filled, 1)
            dve.tensor_tensor(cols[:, BQ1:BV1 + 1, :], cols[:, BQ1:BV1 + 1, :],
                              ST[0][:, 0:3 * C].rearrange("p (v c) -> p v c", c=C), ALU.add)\
               .then_inc(bias_columns_added, 1)
            dve.wait_ge(bias_columns_added, 1)
            for c in range(C):
                dve.tensor_scalar(bv_wide[:, c, :], bv_wide[:, c, :], cols[:, BV1, c:c + 1], None,
                                  ALU.add).then_inc(bv_widened, 1)

            for raw in raw_weights[3:]:
                for c in range(C):
                    dve.tensor_scalar(raw[:, c, :], raw[:, c, :], cols[:, G0, c:c + 1], None, ALU.mult).then_inc(weight_scaled, 1)
            for n, ((high, low), raw) in enumerate(zip(split_weights, raw_weights)):
                dve.wait_ge(weight_high, n + 1)
                dve.tensor_tensor(low[:], raw, high[:].bitcast(F32), ALU.subtract)\
                   .then_inc(weight_low, 1)

            def split(ph, c):
                dve.wait_ge(xt_high, ph.j * C + c + 1)
                dve.tensor_tensor(XTL[:, c, :], XT[:, c, :], XTH[:, c, :].bitcast(F32),
                                   ALU.subtract).then_inc(xt_low, 1)

            def wait_high(ph, stage, c):
                nth = [s for s in SCHEDULE if s[0] in SPLIT].index((stage, c))
                dve.wait_ge(hi_written, ph.j * (C * len(SPLIT)) + nth + 1)

            def xn_low(ph, c):
                wait_high(ph, "transpose", c)
                dve.tensor_tensor(XNL[:, c, :], misc_bank(ph, "transpose", c)[:],
                                  XNH[:, c, :].bitcast(F32), ALU.subtract).then_inc(misc_drained["dve"], 1)

            def lo(ph, stage, c, dst, hi_part, bias):
                wait_high(ph, stage, c)
                dve.scalar_tensor_tensor(out=dst[:, c, :], in0=misc_bank(ph, stage, c)[:],
                                         scalar=cols[:, bias, c:c + 1], in1=hi_part[:, c, :].bitcast(F32),
                                         op0=ALU.add, op1=ALU.subtract).then_inc(misc_drained["dve"], 1)

            def clip(ph):
                if ph.back:
                    dve.wait_ge(masked_pool, (ph.i + 1) * masks(False, QUADS - 1))
                dve.tensor_scalar(CLIP[:], ADJ[:], ADJ_MIN, None, ALU.max).then_inc(adj_clipped, 1)

            def bias(ph):
                dve.wait_ge(adj_loaded, ph.j * DMA + DMA)
                dve.tensor_scalar(BIAS[:], ADJ[:], 0.0, MASKED, ALU.is_equal, ALU.mult).then_inc(bias_built, 1)

            def mask(ph, quad, pair):
                dve.wait_ge(adj_clipped, ph.i + 1)
                dve.wait_ge(exp_done, ph.i * TILES + PER_GROUP * quad + 2 * pair + 2)
                w, clipped = mask_operands(quad, pair)
                dve.tensor_tensor(w, w, clipped, ALU.mult).then_inc(masked_dve, 1)

            def max0(ph, t):
                wait_filled(dve, ph, "max0", t)
                dve.tensor_reduce(mx0[:, t:t + 1], misc_bank(ph, "max0", t)[:], AX.X,
                                  ALU.max).then_inc(misc_drained["dve"], 1)

            def mrow0(ph):
                wait_filled(dve, ph, "mrow0")
                dve.tensor_scalar(nm0[:], misc_bank(ph, "mrow0")[0:1, :], MAX_FLOOR, -1.0, ALU.max,
                                  ALU.mult).then_inc(misc_drained["dve"], 1)

            def max1(ph, g, n):
                t, h = divmod(n, PER_GROUP)
                wait_filled(dve, ph, "max1", g, n)
                dve.tensor_reduce(mx1[:, g, h, t:t + 1], misc_bank(ph, "max1", g, n)[:], AX.X,
                                  ALU.max, negate=True).then_inc(misc_drained["dve"], 1)

            def mrow1(ph, g):
                wait_filled(dve, ph, "mrow1", g)
                dve.tensor_copy(nm1[g][:], misc_bank(ph, "mrow1", g)[0:MAXIMA, 0:P])\
                   .then_inc(misc_drained["dve"], 1)

            def context0(ph, t):
                base = ph.j * FRONT_STEPS
                bank = misc_bank(ph, "context0", t)
                wait_filled(dve, ph, "context0", t)
                if t == 0:
                    dve.wait_ge(x_loaded, ph.j * DMA + DMA)
                dve.tensor_scalar(den0[:, t:t + 1], bank[:, D:D + 1], TINY, None, ALU.max).then_inc(front_step, 1)
                dve.wait_ge(front_step, base + 2 * t + 1)
                dve.reciprocal(rden0[:, t:t + 1], den0[:, t:t + 1]).then_inc(front_step, 1)
                dve.wait_ge(front_step, base + 2 * t + 2)
                dve.scalar_tensor_tensor(out=X[:, t, :], in0=bank[:, 0:D], scalar=rden0[:, t:t + 1],
                                         in1=X[:, t, :], op0=ALU.mult, op1=ALU.add)\
                   .then_inc(misc_drained["dve"], 1)
                wait_drained(dve, ph, "context0", t)
                dve.bn_stats(st0[:, t, :], X[:, t, :]).then_inc(stats_step, 1)

            def stats0(ph):
                dve.wait_ge(stats_step, ph.j * T + T)
                dve.memset(scratch[:], 0.0)
                for t in range(T):
                    dve.bn_aggr(mv0[:, t, :], st0[:, t, :]).then_inc(stats0_ready, 1)

            def norm0(ph):
                dve.wait_ge(rstd0_ready, ph.j + 1)
                if ph.back:
                    dve.wait_ge(res_ready, ph.i + 1)
                for t in range(T):
                    dve.tensor_scalar(xn[:, t, :], X[:, t, :], mv0[:, t, 0:1], rstd0[:, t:t + 1],
                                      ALU.subtract, ALU.mult).then_inc(xn_ready, 1)

            def graph(ph, g):
                return ph.t if g == GROUPS - 1 else ph.i

            def reciprocal(ph, g, part):
                if part == 0:
                    dve.wait_ge(sums_out, (graph(ph, g) * GROUPS + g) * 2 + 2)
                q = slice(P * part, P * (part + 1))
                dve.reciprocal(rden1[:, q], sums_w[:, q]).then_inc(back_step, 1)

            def normalise(ph, g):
                dve.wait_ge(back_step, graph(ph, g) * BACK_STEPS + (g + 1) * T)
                dve.tensor_tensor(OT[:, g, :], sums_v[:], rden1[:], ALU.mult).then_inc(normalised, 1)

            def add_residual(ph):
                dve.wait_ge(res_ready, ph.t + 1)
                dve.wait_ge(out_stored, ph.t * DMA + 1)
                for n, bank in enumerate((PV, DEN)):
                    dve.wait_ge(proj_filled, ph.t * 2 + n + 1)
                    dve.tensor_tensor(z[:, 2 * n:2 * n + 2, :], bank[:].rearrange("p (t e) -> p t e", t=2),
                                      res[:, 2 * n:2 * n + 2, :], ALU.add).then_inc(z_added, 1)

            def stats1(ph):
                dve.wait_ge(z_added, ph.t * 2 + 3)
                for t in range(T):
                    dve.bn_stats(st1[:, t, :], z[:, t, :]).then_inc(tail_step, 1)
                dve.wait_ge(tail_step, ph.t * T + T)
                dve.memset(scratch[:], 0.0)
                for t in range(T):
                    dve.bn_aggr(mv1[:, t, :], st1[:, t, :]).then_inc(stats1_ready, 1)

            def norm1(ph):
                dve.wait_ge(rstd1_ready, ph.t + 1)
                for t in range(T):
                    dve.tensor_scalar(z[:, t, :], z[:, t, :], mv1[:, t, 0:1], rstd1[:, t:t + 1],
                                      ALU.subtract, ALU.mult).then_inc(zn_ready, 1)

            do = {
                "split": split, "clip": clip, "bias": bias,
                "q0": lambda ph, c: lo(ph, "q0", c, Q0L, Q0H, BQ0),
                "k0": lambda ph, c: lo(ph, "k0", c, K0L, K0H, BK0),
                "mask": mask, "max0": max0, "mrow0": mrow0, "context0": context0,
                "stats0": stats0, "norm0": norm0, "stats1": stats1,
                "transpose": xn_low,
                "q1": lambda ph, c: lo(ph, "q1", c, Q1L, Q1H, BQ1),
                "k1": lambda ph, c: lo(ph, "k1", c, K1L, K1H, BK1),
                "max1": max1, "mrow1": mrow1, "reciprocal": reciprocal, "normalise": normalise, "project": add_residual,
                "norm1": norm1,
            }
            run(dve, lambda ph: follow(ph, do))

        @block.gpsimd
        def _(pool):
            POOL_STEPS0 = 1
            POOL_STEPS1 = 2

            pool.memset(z[:, 0, 0:1], 0.0).then_inc(out_stored, 1)
            pool.memset(ident[:], 0.0).then_inc(ident_zeroed, 1)
            pool.wait_ge(ident_zeroed, 1)
            pool.affine_select(out=ident[:], in_=ident[:], compare_op=ALU.not_equal, fill=1.0, base=0,
                               pattern=[[-1, P]], channel_multiplier=1).then_inc(ident_ready, 1)
            pool.wait_ge(consts_set, CONSTS)
            pool.wait_ge(spread_ready, 4)

            def all_rows(n):
                return spread[:, n, :].unsqueeze(1).broadcast_to([P, T, D])

            def residual(ph):
                pool.wait_ge(xn_ready, ph.i * T + T)
                pool.tensor_tensor(res[:], xn[:], all_rows(S_G0), ALU.mult).then_inc(res_step, 1)
                pool.wait_ge(res_step, ph.i + 1)
                pool.tensor_tensor(res[:], res[:], all_rows(S_RES), ALU.add).then_inc(res_ready, 1)

            def rstd(var, ve, dst, step_sem, before, done):
                pool.tensor_tensor(ve[:], var, eps[:], ALU.add).then_inc(step_sem, 1)
                pool.wait_ge(step_sem, before + 1)
                pool.tensor_tensor(dst[:], ve[:], minus_half[:], ALU.pow).then_inc(done, 1)

            def mask(ph, quad, pair):
                if (quad, pair) in DVE_MASKS:
                    return
                if quad == 0 and pair == 0:
                    pool.wait_ge(adj_clipped, ph.i + 1)
                pool.wait_ge(exp_done, ph.i * TILES + PER_GROUP * quad + 2 * pair + 2)
                w, clipped = mask_operands(quad, pair)
                pool.tensor_tensor(w, w, clipped, ALU.mult).then_inc(masked_pool, 1)

            def rstd0_of(ph):
                pool.wait_ge(stats0_ready, ph.j * T + T)
                rstd(mv0[:, :, 1], ve0, rstd0, pool_step0, ph.j * POOL_STEPS0, rstd0_ready)

            def rstd1_of(ph):
                pool.wait_ge(stats1_ready, ph.t * T + T)
                rstd(mv1[:, :, 1], ve1, rstd1, pool_step1, ph.t * POOL_STEPS1, rstd1_ready)

            def output(ph):
                pool.wait_ge(zn_ready, ph.t * T + T)
                pool.tensor_tensor(z[:], z[:], all_rows(S_G1), ALU.mult).then_inc(pool_step1, 1)
                pool.wait_ge(pool_step1, ph.t * POOL_STEPS1 + 2)
                pool.tensor_tensor(z[:], z[:], all_rows(S_B1), ALU.add).then_inc(out_ready, 1)

            do = {"residual": residual, "scores1": mask, "stats0": rstd0_of,
                  "stats1": rstd1_of, "output": output}
            run(pool, lambda ph: follow(ph, do))


def kernel(**inputs):
    import numpy as np
    import concourse.bacc as bacc
    from concourse.bass_utils import run_bass_kernel_spmd

    nc = bacc.Bacc("TRN2", target_bir_lowering=False, num_devices=1)
    arrays, args = {}, []

    def give(name, a):
        a = np.ascontiguousarray(a)
        arrays[name] = a
        args.append(nc.dram_tensor(name, a.shape, mybir.dt.from_np(a.dtype), kind="ExternalInput").ap())

    x, adj = np.asarray(inputs["x"]), np.asarray(inputs["adj"])
    give("x", x)
    give("x_t", x.transpose(0, 2, 1))
    give("adj_t", adj.transpose(0, 2, 1))
    for name in ("L0_gnn_Wq", "L0_gnn_Wk", "L0_gnn_Wc"):
        give(name, np.asarray(inputs[name]))
    for name in ("L1_gnn_Wq", "L1_gnn_Wk", "L1_gnn_Wv", "L1_gnn_Wo"):
        give(name, np.asarray(inputs[name]).T)
    cols = np.stack([np.asarray(inputs[name]) for name in COLS])
    give("channel_cols", cols.reshape(len(COLS), -1, P).transpose(2, 0, 1))
    give("channel_rows", np.stack([np.asarray(inputs[name]) for name in ROWS])[None])
    args.append(nc.dram_tensor("out", x.shape, mybir.dt.from_np(x.dtype), kind="ExternalOutput").ap())
    two_layer_graph_attention(nc, *args)
    r = run_bass_kernel_spmd(nc, [arrays], core_ids=[0])
    return r.results[0]["out"]
```

```python
from contextlib import ExitStack

import concourse.bass as bass
from concourse import mybir

F32 = mybir.dt.float32
F32R = mybir.dt.float32r
BF16 = mybir.dt.bfloat16
ALU = mybir.AluOpType
ACT = mybir.ActivationFunctionType
AX = mybir.AxisListType

P = 128
HEADS = 8
PER_GROUP = 4
GROUPS = HEADS // PER_GROUP
MASKED = -1e18
MAX_FLOOR = -1e17
ADJ_MIN = 1e-8
WEIGHT_BUFFERS = 3
LN_EPS = 1e-5
TINY = 1e-30
DMA = 16


class Phase:

    def __init__(self, t, i, j):
        self.t, self.i, self.j = t, i, j
        self.tail, self.back, self.front = (n is not None for n in (t, i, j))
        self.kind = ("steady" if self.front else "last") if self.back else ("first" if self.front else "end")


def maxima(group, *range_):
    return [("max1", group, n) for n in range(*range_)]


SCHEDULE = (
    [("split", 0), ("split", 1)] + maxima(1, 0, 2) + [("q0", 0), ("reciprocal", 1, 0)]
    + [("q0", 1), ("scores1", 0, 0), ("reciprocal", 1, 1), ("k0", 0), ("scores1", 0, 1)]
    + [("bias",), ("k0", 1), ("scores1", 1, 0), ("reciprocal", 1, 2), ("u", 0), ("scores1", 1, 1)]
    + [("reciprocal", 1, 3), ("max0", 0), ("max0", 1), ("max0", 2), ("max0", 3), ("normalise", 1), ("high_output", 1)]
    + [("u", 1), ("mrow0",), ("low_output", 1)] + maxima(1, 2, 4) + [("project",), ("values1", 0)]
    + maxima(1, 4, 5) + [("stats1",), ("denominators1", 0)] + maxima(1, 5, 6)
    + [("scores0", 0), ("norm1",), ("scores1", 2, 0)] + maxima(1, 6, 8)
    + [("scores0", 1), ("prepare", 0), ("scores1", 2, 1), ("output",), ("values1", 1)]
    + maxima(1, 8, 10) + [("scores0", 2), ("scores1", 3, 0)] + maxima(1, 10, 12) + [("denominators1", 1)]
    + [("scores1", 3, 1), ("scores0", 3), ("prepare", 1), ("skip_back",)] + maxima(1, 12, 14) + [("residual",), ("values1", 2)]
    + maxima(1, 14, 16) + [("context0", 0), ("skip_back",), ("denominators1", 2), ("mrow1", 1)]
    + [("context0", 1), ("values1", 3), ("scores1", 4, 0), ("mask", 4, 0), ("context0", 2)]
    + [("scores1", 4, 1), ("denominators1", 3), ("sums_out", 0), ("context0", 3), ("skip_back",), ("scores1", 5, 0)]
    + [("values1", 4), ("stats0",), ("mask", 5, 0), ("norm0",), ("scores1", 5, 1), ("denominators1", 4), ("scores1", 6, 0)]
    + [("transpose", 0), ("transpose", 1), ("reciprocal", 0, 0), ("reciprocal", 0, 1), ("reciprocal", 0, 2), ("reciprocal", 0, 3)]
    + [("scores1", 6, 1), ("values1", 5), ("denominators1", 5), ("q1", 0), ("normalise", 0), ("k1", 0), ("high_output", 0)]
    + [("scores1", 7, 0), ("values1", 6)] + maxima(0, 0, 3) + [("low_output", 0), ("q1", 1)] + maxima(0, 3, 6)
    + [("scores1", 7, 1), ("denominators1", 6)] + maxima(0, 6, 9) + [("k1", 1)] + maxima(0, 9, 12)
    + [("values1", 7), ("clip",)] + maxima(0, 12, 14) + [("denominators1", 7), ("sums_out", 1), ("v", 0)]
    + maxima(0, 14, 16) + [("v", 1), ("mrow1", 0), ("prepare", 2)]
)

DVE_MASKS = [s[1:] for s in SCHEDULE if s[0] == "mask"]


def masks(by_dve, quad):
    n = sum(1 for q, _ in DVE_MASKS if q <= quad)
    return n if by_dve else 2 * quad + 2 - n


MISC_BANKS = 4
MISC_DRAIN = {
    "q0": "dve", "k0": "dve", "u": "act", "max0": "dve", "mrow0": "dve", "scores0": "act",
    "context0": "dve", "transpose": "dve", "q1": "dve", "k1": "dve", "v": "act", "max1": "dve",
    "mrow1": "dve",
    "skip_back": None,
}
BACK = ("residual", "mask", "scores1", "values1", "denominators1", "sums_out",
        "reciprocal", "normalise", "high_output", "low_output", "skip_back")
TAIL = ("project", "stats1", "norm1", "output")
SPLIT = ("q0", "k0", "transpose", "q1", "k1")


def is_back(stage):
    return stage[0] in BACK or stage[:2] in (("max1", 1), ("mrow1", 1))


def is_tail(stage):
    return stage[0] in TAIL or stage[:2] in [
        (s, GROUPS - 1) for s in ("reciprocal", "normalise", "high_output", "low_output")]


def stages(ph):
    def present(stage):
        if stage[0] == "prepare":
            return ph.kind == "first"
        return ph.tail if is_tail(stage) else ph.back if is_back(stage) else ph.front

    return [s for s in SCHEDULE if present(s)]


class MiscBanks:

    def __init__(self, graphs):
        self.uses = {ph.kind: [s for s in stages(ph) if s[0] in MISC_DRAIN]
                     for ph in (Phase(None, None, 0), Phase(0, 1, 2), Phase(0, 1, None))}
        assert all(len(self.uses[k]) % MISC_BANKS == 0 for k in ("first", "steady"))
        self.graphs = graphs

    @staticmethod
    def _number(uses, what):
        return sum(1 for s in uses if MISC_DRAIN[s[0]] and what in ("fill", MISC_DRAIN[s[0]]))

    def _base(self, ph, what):
        first, steady = (self._number(self.uses[k], what) for k in ("first", "steady"))
        if ph.kind == "first":
            return 0
        return (ph.i if ph.kind == "steady" else self.graphs - 1) * steady + first

    def bank(self, ph, *stage):
        return self.uses[ph.kind].index(stage) % MISC_BANKS

    def count(self, ph, what, *stage):
        uses = self.uses[ph.kind]
        return self._base(ph, what) + self._number(uses[: uses.index(stage) + 1], what)

    def count_before(self, ph, *stage):
        uses, e = self.uses["steady"], MISC_DRAIN[stage[0]]
        later = [s for s in uses[uses.index(stage) + 1:] if MISC_DRAIN[s[0]] == e]
        assert not any(map(is_back, later))
        return self._base(ph, e) - self._number(later, e)

    def before(self, ph, *stage):
        uses = self.uses[ph.kind]
        n = uses.index(stage) - MISC_BANKS
        while n >= 0 and MISC_DRAIN[uses[n][0]] is None:
            n -= MISC_BANKS
        if n >= 0:
            e = MISC_DRAIN[uses[n][0]]
            return e, self.count(ph, e, *uses[n])
        if ph.kind == "first":
            return None
        use = self.uses["steady"][n]
        e = MISC_DRAIN[use[0]]
        return e, self.count_before(ph, *use)


COLS = ("L0_gnn_bq", "L0_gnn_bk", "L1_gnn_bq", "L1_gnn_bk", "L1_gnn_bv", "L0_gnn_gamma", "L0_gnn_beta")
ROWS = ("L0_gnn_gamma", "L0_gnn_beta", "L1_gnn_bo", "L1_gnn_gamma", "L1_gnn_beta")


def two_layer_graph_attention(nc, x, x_t, adj_t, wq0, wk0, wc0, wq1_t, wk1_t, wv1_t, wo1_t,
                              channel_cols, channel_rows, out):
    B, N, D = x.shape
    T = N // P
    C = D // P
    DK = D // HEADS
    SCALE0 = float(D) ** -0.5
    SCALE1 = float(DK) ** -0.5
    assert (T, C, DK, GROUPS) == (4, 2, 32, C) and HEADS * DK == D
    HI_HI, HI_LO, LO_HI, MROW = 0, DK, 2 * DK, 3 * DK
    STACK = 3 * DK + 1
    MAXIMA = PER_GROUP * T
    TILES = HEADS * T
    PAIRS = TILES // 2
    QUADS = GROUPS * T
    STACK_DMAS = 6 * PER_GROUP

    misc = MiscBanks(B)

    with ExitStack() as ctx:
        def sb(name, shape, dt=F32):
            return ctx.enter_context(nc.sbuf_tensor(name, shape, dt))

        def ps(name, shape):
            return ctx.enter_context(nc.psum_tensor(name, shape, F32))

        def sem(name):
            return ctx.enter_context(nc.semaphore(name))

        ident = sb("ident", [P, P])
        ident_bf = sb("ident_bf", [P, P], BF16)
        ones = sb("ones", [P, P])
        ones_r = sb("ones_r", [1, P], F32R)
        minus_half = sb("minus_half", [P, T])
        eps = sb("eps", [P, T])
        scratch = sb("scratch", [P, 1])
        split_weights = [tuple(sb(n + part, [P, C, D], F32R) for part in ("_high", "_low"))
                         for n in ("Wq0", "Wk0", "Wc0", "Wq1", "Wk1", "Wv1", "Wo1")]
        Wq0, Wk0, Wc0, Wq1, Wk1, Wv1, Wo1 = split_weights
        SCALED = range(3, 6)
        cols = sb("cols", [P, len(COLS), C])
        BQ0, BK0, BQ1, BK1, BV1, G0, B0 = range(len(COLS))
        R_G0, R_B0, R_BO, R_G1, R_B1 = range(len(ROWS))
        spread = sb("spread", [P, 4, D])
        S_G0, S_RES, S_G1, S_B1 = range(4)

        X = sb("X", [P, T, D])
        XTH, XTL = (sb(n, [P, C, N], F32R) for n in ("XTH", "XTL"))
        ADJ = sb("ADJ", [P, T, N])
        BIAS = sb("BIAS", [P, T, N], BF16)
        Q0H, Q0L, K0H, K0L = (sb(n, [P, C, N], F32R) for n in ("Q0H", "Q0L", "K0H", "K0L"))
        U = sb("U", [P, T, D + 1])
        mx0 = sb("mx0", [P, T])
        nm0 = sb("nm0", [1, N], F32R)
        P0 = sb("P0", [P, T, N])
        XT = P0[:, 0:C, :]
        den0 = sb("den0", [P, T])
        rden0 = sb("rden0", [P, T])
        st0 = sb("st0", [P, T, 6])
        mv0 = sb("mv0", [P, T, 2])
        ve0 = sb("ve0", [P, T])
        rstd0 = sb("rstd0", [P, T])
        xn = sb("xn", [P, T, D])
        XNH, XNL = (sb(n, [P, C, N], F32R) for n in ("XNH", "XNL"))
        Q1H, Q1L, K1H, K1L = (sb(n, [P, C, N], F32R) for n in ("Q1H", "Q1L", "K1H", "K1L"))
        mx1 = sb("mx1", [P, GROUPS, PER_GROUP, T])
        nm1 = [sb(f"nm1_{g}", [MAXIMA, P], F32R) for g in range(GROUPS)]
        QS = sb("QS", [STACK, HEADS, N], F32R)
        KS = sb("KS", [STACK, HEADS, N], F32R)

        V = sb("V", [P, T, D])
        CLIP = sb("CLIP", [P, T, N])
        PR = [sb(f"PR{n}", [P, PER_GROUP, N]) for n in range(WEIGHT_BUFFERS)]
        sums_v = sb("sums_v", [P, N])
        sums_w = sb("sums_w", [P, N])
        raw_weights = [PR[n // PER_GROUP][:, n % PER_GROUP, :].rearrange("p (c e) -> p c e", c=C)
                       for n in range(len(split_weights))]
        flat = PR[2][:].rearrange("p t n -> p (t n)")
        rows = flat[0:1, 0:len(ROWS) * D].rearrange("p (v e) -> p v e", e=D)
        bv_wide = flat[:, len(ROWS) * D:len(ROWS) * D + C * P].rearrange("p (c q) -> p c q", q=P)
        OTH, OTL = (sb(n, [P, C, N], F32R) for n in ("OTH", "OTL"))
        res = sb("res", [P, T, D])
        z = sb("z", [P, T, D])
        st1 = sb("st1", [P, T, 6])
        mv1 = sb("mv1", [P, T, 2])
        ve1 = sb("ve1", [P, T])
        rstd1 = sb("rstd1", [P, T])

        MISC = [ps(f"misc{n}", [P, N]) for n in range(MISC_BANKS)]
        ST = [ps(f"scores{n}", [P, N]) for n in range(2)]
        PV = ps("values", [P, N])
        DEN = ps("denominators", [P, N])

        SPREAD_BANKS = [bank[:, D * half:D * (half + 1)] for bank in (ST[1], PV) for half in range(2)]

        first_loaded = sem("first_loaded")
        rest_loaded = sem("rest_loaded")
        consts_set = sem("consts_set")
        ident_zeroed = sem("ident_zeroed")
        ident_ready = sem("ident_ready")
        bv_widened = sem("bv_widened")
        spread_filled = sem("spread_filled")
        spread_ready = sem("spread_ready")
        bias_columns_filled = sem("bias_columns_filled")
        bias_columns_added = sem("bias_columns_added")
        weight_scaled = sem("weight_scaled")
        weight_high = sem("weight_high")
        weight_low = sem("weight_low")
        x_loaded = sem("x_loaded")
        xt_loaded = sem("xt_loaded")
        xt_high = sem("xt_high")
        xt_low = sem("xt_low")
        adj_loaded = sem("adj_loaded")
        misc_filled = sem("misc_filled")
        misc_drained = {"act": sem("misc_drained_act"), "dve": sem("misc_drained_dve")}
        hi_written = sem("hi_written")
        bias_built = sem("bias_built")
        adj_clipped = sem("adj_clipped")
        front_step = sem("front_step")
        stats_step = sem("stats_step")
        back_step = sem("back_step")
        tail_step = sem("tail_step")
        stats0_ready = sem("stats0_ready")
        rstd0_ready = sem("rstd0_ready")
        xn_ready = sem("xn_ready")
        pool_step0 = sem("pool_step0")
        res_step = sem("res_step")
        pool_step1 = sem("pool_step1")
        stack_loaded = [sem(f"stack_loaded{g}") for g in range(GROUPS)]
        mrow_loaded = [sem(f"mrow_loaded{g}") for g in range(GROUPS)]
        scores_filled = sem("scores_filled")
        exp_done = sem("exp_done")
        masked_pool = sem("masked_pool")
        masked_dve = sem("masked_dve")
        quad_summed = sem("quad_summed")
        sums_out = sem("sums_out")
        normalised = sem("normalised")
        output_high = sem("output_high")
        output_low = sem("output_low")
        proj_filled = sem("proj_filled")
        z_added = sem("z_added")
        stats1_ready = sem("stats1_ready")
        rstd1_ready = sem("rstd1_ready")
        zn_ready = sem("zn_ready")
        res_ready = sem("res_ready")
        out_ready = sem("out_ready")
        out_stored = sem("out_stored")

        FIRST_LOADS, REST_LOADS = 3 + 1, 4 + 1
        CONSTS = 7
        block = ctx.enter_context(nc.Block())

        def misc_bank(ph, *stage):
            return MISC[misc.bank(ph, *stage)]

        def wait_drained(eng, ph, *stage):
            e = MISC_DRAIN[stage[0]]
            eng.wait_ge(misc_drained[e], misc.count(ph, e, *stage))

        def wait_filled(eng, ph, *stage):
            eng.wait_ge(misc_filled, misc.count(ph, "fill", *stage))

        def graph_of(ph, g):
            return ph.t if g == GROUPS - 1 else ph.i

        def mask_operands(quad, pair):
            w = PR[quad % WEIGHT_BUFFERS][:, 2 * pair:2 * pair + 2, :]
            return w, CLIP[:, quad % T, :].unsqueeze(1).broadcast_to([P, 2, N])

        def run(eng, step):
            step(Phase(None, None, 0))
            step(Phase(None, 0, 1))
            with eng.Fori(1, B - 1) as i:
                step(Phase(i - 1, i, i + 1))
            step(Phase(B - 2, B - 1, None))
            step(Phase(B - 1, None, None))

        def follow(ph, do):
            for stage, *where in stages(ph):
                if stage in do:
                    do[stage](ph, *where)

        @block.sync
        def _(sp):
            def load_stacks(g):
                for h in range(PER_GROUP):
                    part = slice(DK * h, DK * (h + 1))
                    for stack, parts in ((QS, (Q1H, Q1H, Q1L)), (KS, (K1H, K1L, K1H))):
                        for row, src in zip((HI_HI, HI_LO, LO_HI), parts):
                            sp.dma_start(stack[row:row + DK, PER_GROUP * g + h, :].bitcast(F32),
                                         src[part, g, :].bitcast(F32)).then_inc(stack_loaded[g], DMA)

            def load_mrow(g):
                row = QS[MROW:STACK, PER_GROUP * g:PER_GROUP * (g + 1), :].bitcast(F32)
                sp.dma_start(row.rearrange("o h (t q) -> o (h t) q", q=P),
                             nm1[g][:].bitcast(F32)).then_inc(mrow_loaded[g], DMA)

            def load_xt(j):
                sp.dma_start(XT, x_t[j].rearrange("(c p) n -> p c n", p=P)).then_inc(xt_loaded, DMA)

            def load_x(j):
                sp.dma_start(X[:], x[j].rearrange("(t p) e -> p t e", p=P)).then_inc(x_loaded, DMA)

            def load_adj(j):
                sp.dma_start(ADJ[:], adj_t[j].rearrange("(t p) q -> p t q", p=P)).then_inc(adj_loaded, DMA)

            def load_second_mrow(ph):
                wait_drained(sp, ph, "mrow1", 1)
                load_mrow(1)

            def store(i):
                sp.wait_ge(out_ready, i + 1)
                sp.dma_start(out[i].rearrange("(t p) e -> p t e", p=P), z[:]).then_inc(out_stored, DMA)

            def finish_front(ph):
                i, j = ph.i, ph.j
                sp.wait_ge(misc_drained["dve"], misc.count_before(ph, "k1", 0))
                if ph.front:
                    load_xt(j)
                load_stacks(0)
                sp.wait_ge(misc_drained["dve"], misc.count_before(ph, "mrow1", 0))
                load_mrow(0)
                if ph.front:
                    sp.wait_ge(adj_clipped, i + 1)
                    load_adj(j)
                load_stacks(1)
                if ph.front:
                    load_x(j)

            load_xt(0)
            sp.dma_start(cols[:], channel_cols).then_inc(first_loaded, DMA)
            for w, src in zip(raw_weights[:3], (wq0, wk0, wc0)):
                sp.dma_start(w, src.rearrange("(c p) e -> p c e", p=P)).then_inc(first_loaded, DMA)
            load_adj(0)
            for w, src in zip(raw_weights[3:], (wq1_t, wk1_t, wv1_t, wo1_t)):
                sp.dma_start(w, src.rearrange("(c p) e -> p c e", p=P)).then_inc(rest_loaded, DMA)
            sp.dma_start(rows, channel_rows).then_inc(rest_loaded, DMA)
            load_x(0)
            first = Phase(None, 0, 1)
            finish_front(first)
            load_second_mrow(first)
            with sp.Fori(1, B - 1) as i:
                ph = Phase(i - 1, i, i + 1)
                finish_front(ph)
                store(i - 1)
                load_second_mrow(ph)
            last = Phase(B - 2, B - 1, None)
            finish_front(last)
            store(B - 2)
            load_second_mrow(last)
            store(B - 1)
            sp.wait_ge(out_stored, B * DMA + 1)

        @block.tensor
        def _(pe):
            def fill(ph, *stage):
                before = misc.before(ph, *stage)
                if before is not None:
                    pe.wait_ge(misc_drained[before[0]], before[1])
                return misc_bank(ph, *stage)

            pe.wait_ge(consts_set, CONSTS)
            pe.wait_ge(ident_ready, 2)

            def prepare(ph, part):
                if part == 0:
                    pe.wait_ge(rest_loaded, REST_LOADS * DMA)
                    for n, w in enumerate(raw_weights[m] for m in SCALED):
                        for c in range(C):
                            for k in range(C):
                                mm = pe.matmul(ST[0][:, C * n + c:C * n + c + 1],
                                               w[:, k, P * c:P * (c + 1)], cols[:, B0, k:k + 1],
                                               start=(k == 0), stop=(k == C - 1))
                    mm.then_inc(bias_columns_filled, 1)
                elif part == 1:
                    pe.wait_ge(bv_widened, C)
                    one = ones[0:1, :]
                    pe.matmul(SPREAD_BANKS[S_G0], one, rows[:, R_G0, :], start=True, stop=True)
                    for n in (R_B0, R_BO):
                        pe.matmul(SPREAD_BANKS[S_RES], one, rows[:, n, :], start=(n == R_B0), stop=False)
                    for c in range(C):
                        pe.matmul(SPREAD_BANKS[S_RES], bv_wide[:, c, :], raw_weights[-1][:, c, :], start=False,
                                  stop=(c == C - 1))
                    pe.matmul(SPREAD_BANKS[S_G1], one, rows[:, R_G1, :], start=True, stop=True)
                    pe.matmul(SPREAD_BANKS[S_B1], one, rows[:, R_B1, :], start=True, stop=True)\
                      .then_inc(spread_filled, 1)
                else:
                    pe.wait_ge(spread_ready, 4)

            def products(weights, src):
                return [(w, s, k) for w, s in ((weights[0], src[0]), (weights[1], src[0]), (weights[0], src[1]))
                        for k in range(C)]

            def project(ph, stage, c, weights, src, wait_for=None):
                wait_for_weights(ph, weights, c == 0)
                bank = fill(ph, stage, c)
                terms = products(weights, src)
                for n, (w, s, k) in enumerate(terms):
                    if wait_for:
                        wait_for(s, k)
                    mm = pe.matmul(bank[:], w[:, k, P * c:P * (c + 1)], s[:, k, :],
                                   start=(n == 0), stop=(n == len(terms) - 1))
                mm.then_inc(misc_filled, 1)

            def project_rows(ph, stage, m, weights, src):
                wait_for_weights(ph, weights, m == 0)
                bank = fill(ph, stage, m)
                terms = products(weights, src)
                for half in range(2):
                    t = 2 * m + half
                    for n, (w, s, k) in enumerate(terms):
                        mm = pe.matmul(bank[:, D * half:D * (half + 1)], s[:, k, P * t:P * (t + 1)],
                                       w[:, k, :], start=(n == 0), stop=(n == len(terms) - 1))
                mm.then_inc(misc_filled, 1)

            X_PARTS, XN_PARTS = (XTH, XTL), (XNH, XNL)

            def wait_for_weights(ph, weights, first):
                if ph.kind == "first" and first:
                    pe.wait_ge(weight_low, split_weights.index(weights) + 1)

            def q0(ph, c):
                def wait_for_x(part, k):
                    pe.wait_ge(xt_high if part is XTH else xt_low, ph.j * C + k + 1)

                project(ph, "q0", c, Wq0, X_PARTS, wait_for_x if c == 0 else None)

            def q1(ph, c):
                if c == 0:
                    wait_drained(pe, ph, "transpose", 1)
                project(ph, "q1", c, Wq1, XN_PARTS)

            def max0(ph, t):
                if t == 0:
                    wait_drained(pe, ph, "k0", 1)
                    pe.wait_ge(bias_built, ph.j + 1)
                bank = fill(ph, "max0", t)
                q = slice(P * t, P * (t + 1))
                for c in range(C):
                    pe.matmul(bank[:], Q0H[:, c, q], K0H[:, c, :], start=(c == 0), stop=False)
                for k in range(T):
                    mm = pe.matmul(bank[:, P * k:P * (k + 1)], BIAS[:, k, q], ident_bf[:],
                                   start=False, stop=(k == T - 1))
                mm.then_inc(misc_filled, 1)

            def mrow0(ph):
                wait_drained(pe, ph, "max0", T - 1)
                bank = fill(ph, "mrow0")
                for t in range(T):
                    mm = pe.matmul(bank[0:1, P * t:P * (t + 1)], mx0[:, t:t + 1], ident[:],
                                   start=True, stop=True)
                mm.then_inc(misc_filled, 1)

            def scores0(ph, k):
                if k == 0:
                    wait_drained(pe, ph, "mrow0")
                bank = fill(ph, "scores0", k)
                rows_k = slice(P * k, P * (k + 1))
                n = 0
                for c in range(C):
                    for kk, qq in ((K0H, Q0H), (K0L, Q0H), (K0H, Q0L)):
                        pe.matmul(bank[:], kk[:, c, rows_k], qq[:, c, :], start=(n == 0), stop=False)
                        n += 1
                pe.matmul(bank[:], ones_r[:], nm0[:], start=False, stop=False)
                pe.matmul(bank[:], ident_bf[:], BIAS[:, k, :], start=False, stop=True).then_inc(misc_filled, 1)

            def context0(ph, t):
                if t == 0:
                    wait_drained(pe, ph, "scores0", T - 1)
                bank = fill(ph, "context0", t)
                for k in range(T):
                    mm = pe.matmul(bank[:, 0:D + 1], P0[:, k, P * t:P * (t + 1)], U[:, k, :],
                                   start=(k == 0), stop=(k == T - 1))
                mm.then_inc(misc_filled, 1)

            def transpose(ph, c):
                bank = fill(ph, "transpose", c)
                for t in range(T):
                    if c == 0:
                        pe.wait_ge(xn_ready, ph.j * T + t + 1)
                    mm = pe.transpose(bank[:, P * t:P * (t + 1)], xn[:, t, P * c:P * (c + 1)], ident[:])
                mm.then_inc(misc_filled, 1)

            def max1(ph, g, n):
                if n == 0 and g == 0:
                    wait_drained(pe, ph, "k1", 0)
                elif n == 0:
                    pe.wait_ge(misc_drained["dve"], misc.count_before(ph, "k1", 1))
                bank = fill(ph, "max1", g, n)
                t, h = divmod(n, PER_GROUP)
                part = slice(DK * h, DK * (h + 1))
                pe.matmul(bank[:], Q1H[part, g, P * t:P * (t + 1)], K1H[part, g, :],
                          start=True, stop=True).then_inc(misc_filled, 1)

            def mrow1(ph, g):
                wait_drained(pe, ph, "max1", g, PER_GROUP * T - 1)
                pe.matmul(fill(ph, "mrow1", g)[0:MAXIMA, 0:P], mx1[:, g, :, :].rearrange("p h t -> p (h t)"),
                          ident[:], start=True, stop=True).then_inc(misc_filled, 1)

            def scores1(ph, quad, pair):
                g, k = divmod(quad, T)
                if k == 0 and pair == 0:
                    pe.wait_ge(stack_loaded[g], (ph.i + 1) * (STACK_DMAS * DMA))
                    pe.wait_ge(mrow_loaded[g], (ph.i + 1) * DMA)
                for n in range(2):
                    tile = PER_GROUP * quad + 2 * pair + n
                    if tile >= 2:
                        pe.wait_ge(exp_done, ph.i * TILES + tile - 1)
                    h = PER_GROUP * g + 2 * pair + n
                    pe.matmul(ST[n][:], KS[:, h, P * k:P * (k + 1)], QS[:, h, :],
                              start=True, stop=True).then_inc(scores_filled, 1)

            def sums1(ph, quad, bank, first):
                g, k = divmod(quad, T)
                if quad == 0 and ph.tail:
                    pe.wait_ge(z_added, ph.t * 2 + (1 if bank is PV else 2))
                if first:
                    pe.wait_ge(masked_pool, ph.i * masks(False, QUADS - 1) + masks(False, quad))
                    if any(q == quad for q, _ in DVE_MASKS):
                        pe.wait_ge(masked_dve, ph.i * len(DVE_MASKS) + masks(True, quad))
                    if quad == 0:
                        pe.wait_ge(misc_drained["act"], misc.count_before(ph, "v", 1))
                    elif k == 0:
                        pe.wait_ge(sums_out, (ph.i * GROUPS + g) * 2)
                for h in range(PER_GROUP):
                    c = DK * (PER_GROUP * g + h)
                    w = V[:, k, c:c + DK] if bank is PV else ones[:, 0:DK]
                    mm = pe.matmul(bank[DK * h:DK * (h + 1), :], w, PR[quad % WEIGHT_BUFFERS][:, h, :],
                                   start=(k == 0), stop=(k == T - 1))
                return mm

            def values_first(quad):
                return SCHEDULE.index(("values1", quad)) < SCHEDULE.index(("denominators1", quad))

            def values1(ph, quad):
                first = values_first(quad)
                mm = sums1(ph, quad, PV, first)
                if not first:
                    mm.then_inc(quad_summed, 1)

            def denominators1(ph, quad):
                first = not values_first(quad)
                mm = sums1(ph, quad, DEN, first)
                if not first:
                    mm.then_inc(quad_summed, 1)

            def project_out(ph):
                terms = products(Wo1, (OTH, OTL))
                pe.wait_ge(output_high, ph.t * GROUPS + GROUPS)
                for t in range(T):
                    bank = (PV, DEN)[t // 2]
                    for n, (w, s, k) in enumerate(terms):
                        if t == 0 and s is OTL:
                            pe.wait_ge(output_low, ph.t * GROUPS + k + 1)
                        mm = pe.matmul(bank[:, D * (t % 2):D * (t % 2 + 1)], s[:, k, P * t:P * (t + 1)],
                                       w[:, k, :], start=(n == 0), stop=(n == len(terms) - 1))
                    if t % 2:
                        mm.then_inc(proj_filled, 1)

            do = {
                "prepare": prepare, "q0": q0,
                "k0": lambda ph, c: project(ph, "k0", c, Wk0, X_PARTS),
                "u": lambda ph, n: project_rows(ph, "u", n, Wc0, X_PARTS),
                "max0": max0, "mrow0": mrow0, "scores0": scores0, "context0": context0,
                "transpose": transpose, "q1": q1,
                "k1": lambda ph, c: project(ph, "k1", c, Wk1, XN_PARTS),
                "v": lambda ph, n: project_rows(ph, "v", n, Wv1, XN_PARTS),
                "max1": max1, "mrow1": mrow1, "scores1": scores1, "values1": values1,
                "denominators1": denominators1, "project": project_out,
            }
            run(pe, lambda ph: follow(ph, do))

        @block.scalar
        def _(act):
            def weight_high_part(n):
                act.copy(split_weights[n][0][:], raw_weights[n]).then_inc(weight_high, 1)

            def prepare(ph, part):
                if part == 1:
                    for n in range(3, len(split_weights)):
                        if n in SCALED:
                            act.wait_ge(weight_scaled, (n - 2) * C)
                        weight_high_part(n)
                    act.wait_ge(spread_filled, 1)
                    for n, bank in enumerate(SPREAD_BANKS):
                        act.copy(spread[:, n, :], bank).then_inc(spread_ready, 1)

            act.wait_ge(first_loaded, FIRST_LOADS * DMA)
            for n in range(3):
                weight_high_part(n)

            def split(ph, c):
                if c == 0:
                    act.wait_ge(xt_loaded, ph.j * DMA + DMA)
                act.copy(XTH[:, c, :], XT[:, c, :]).then_inc(xt_high, 1)

            def hi(ph, stage, c, dst, bias):
                wait_filled(act, ph, stage, c)
                act.activation(dst[:, c, :], misc_bank(ph, stage, c)[:], ACT.Identity,
                               bias=cols[:, bias, c:c + 1]).then_inc(hi_written, 1)

            def rows_out(ph, stage, n, dst):
                wait_filled(act, ph, stage, n)
                act.copy(dst[:, 2 * n:2 * n + 2, 0:D],
                         misc_bank(ph, stage, n)[:].rearrange("p (t e) -> p t e", t=2))\
                   .then_inc(misc_drained["act"], 1)

            def exp0(ph, k):
                wait_filled(act, ph, "scores0", k)
                act.activation(P0[:, k, :], misc_bank(ph, "scores0", k)[:], ACT.Exp,
                               scale=SCALE0).then_inc(misc_drained["act"], 1)

            def exp1(ph, quad, pair):
                if quad >= WEIGHT_BUFFERS and pair == 0:
                    act.wait_ge(quad_summed, ph.i * QUADS + quad - WEIGHT_BUFFERS + 1)
                for n in range(2):
                    h = 2 * pair + n
                    act.wait_ge(scores_filled, ph.i * TILES + PER_GROUP * quad + h + 1)
                    act.activation(PR[quad % WEIGHT_BUFFERS][:, h, :], ST[n][:], ACT.Exp,
                                   scale=SCALE1).then_inc(exp_done, 1)

            def copy_sums(ph, g):
                act.wait_ge(quad_summed, ph.i * QUADS + (g + 1) * T)
                if g > 0:
                    act.wait_ge(output_low, ph.i * GROUPS + g)
                act.copy(sums_w[:], DEN[:]).then_inc(sums_out, 1)
                act.copy(sums_v[:], PV[:]).then_inc(sums_out, 1)

            def high_output(ph, g):
                act.wait_ge(normalised, graph_of(ph, g) * GROUPS + g + 1)
                act.copy(OTH[:, g, :], sums_v[:]).then_inc(output_high, 1)

            def xn_high(ph, c):
                wait_filled(act, ph, "transpose", c)
                act.copy(XNH[:, c, :], misc_bank(ph, "transpose", c)[:]).then_inc(hi_written, 1)

            do = {
                "prepare": prepare, "split": split,
                "q0": lambda ph, c: hi(ph, "q0", c, Q0H, BQ0),
                "k0": lambda ph, c: hi(ph, "k0", c, K0H, BK0),
                "u": lambda ph, n: rows_out(ph, "u", n, U),
                "scores0": exp0, "transpose": xn_high,
                "q1": lambda ph, c: hi(ph, "q1", c, Q1H, BQ1),
                "k1": lambda ph, c: hi(ph, "k1", c, K1H, BK1),
                "v": lambda ph, n: rows_out(ph, "v", n, V),
                "scores1": exp1, "sums_out": copy_sums,
                "high_output": high_output,
            }
            run(act, lambda ph: follow(ph, do))

        @block.vector
        def _(dve):
            FRONT_STEPS = 2 * T
            BACK_STEPS = GROUPS * T

            dve.memset(ones[:], 1.0).then_inc(consts_set, 1)
            dve.memset(ones_r[:].bitcast(F32), 1.0).then_inc(consts_set, 1)
            dve.memset(minus_half[:], -0.5).then_inc(consts_set, 1)
            dve.memset(eps[:], LN_EPS).then_inc(consts_set, 1)
            dve.memset(U[:, :, D:D + 1], 1.0).then_inc(consts_set, 1)
            dve.memset(KS[MROW:STACK, :, :].bitcast(F32), 1.0).then_inc(consts_set, 1)
            dve.memset(bv_wide, 0.0).then_inc(consts_set, 1)
            dve.wait_ge(consts_set, CONSTS)
            dve.wait_ge(ident_ready, 1)
            dve.tensor_copy(ident_bf[:], ident[:]).then_inc(ident_ready, 1)

            def weight_low_part(n):
                high, low = split_weights[n]
                dve.wait_ge(weight_high, n + 1)
                dve.tensor_tensor(low[:], raw_weights[n], high[:].bitcast(F32), ALU.subtract)\
                   .then_inc(weight_low, 1)

            def prepare(ph, part):
                if part == 0:
                    dve.wait_ge(bias_columns_filled, 1)
                    dve.tensor_tensor(cols[:, BQ1:BV1 + 1, :], cols[:, BQ1:BV1 + 1, :],
                                      ST[0][:, 0:3 * C].rearrange("p (v c) -> p v c", c=C), ALU.add)\
                       .then_inc(bias_columns_added, 1)
                    dve.wait_ge(bias_columns_added, 1)
                    for c in range(C):
                        dve.tensor_scalar(bv_wide[:, c, :], bv_wide[:, c, :], cols[:, BV1, c:c + 1], None,
                                          ALU.add).then_inc(bv_widened, 1)
                    for n in SCALED:
                        raw = raw_weights[n]
                        for c in range(C):
                            dve.tensor_scalar(raw[:, c, :], raw[:, c, :], cols[:, G0, c:c + 1], None,
                                              ALU.mult).then_inc(weight_scaled, 1)
                elif part == 1:
                    for n in range(3, len(split_weights)):
                        weight_low_part(n)

            for n in range(3):
                weight_low_part(n)

            def split(ph, c):
                dve.wait_ge(xt_high, ph.j * C + c + 1)
                dve.tensor_tensor(XTL[:, c, :], XT[:, c, :], XTH[:, c, :].bitcast(F32),
                                   ALU.subtract).then_inc(xt_low, 1)

            def wait_high(ph, stage, c):
                nth = [s for s in SCHEDULE if s[0] in SPLIT].index((stage, c))
                dve.wait_ge(hi_written, ph.j * (C * len(SPLIT)) + nth + 1)

            def xn_low(ph, c):
                wait_high(ph, "transpose", c)
                dve.tensor_tensor(XNL[:, c, :], misc_bank(ph, "transpose", c)[:],
                                  XNH[:, c, :].bitcast(F32), ALU.subtract).then_inc(misc_drained["dve"], 1)

            def lo(ph, stage, c, dst, hi_part, bias):
                wait_high(ph, stage, c)
                dve.scalar_tensor_tensor(out=dst[:, c, :], in0=misc_bank(ph, stage, c)[:],
                                         scalar=cols[:, bias, c:c + 1], in1=hi_part[:, c, :].bitcast(F32),
                                         op0=ALU.add, op1=ALU.subtract).then_inc(misc_drained["dve"], 1)

            def clip(ph):
                if ph.back:
                    dve.wait_ge(masked_pool, (ph.i + 1) * masks(False, QUADS - 1))
                dve.tensor_scalar(CLIP[:], ADJ[:], ADJ_MIN, None, ALU.max).then_inc(adj_clipped, 1)

            def bias(ph):
                dve.wait_ge(adj_loaded, ph.j * DMA + DMA)
                dve.tensor_scalar(BIAS[:], ADJ[:], 0.0, MASKED, ALU.is_equal, ALU.mult).then_inc(bias_built, 1)

            def mask(ph, quad, pair):
                dve.wait_ge(adj_clipped, ph.i + 1)
                dve.wait_ge(exp_done, ph.i * TILES + PER_GROUP * quad + 2 * pair + 2)
                w, clipped = mask_operands(quad, pair)
                dve.tensor_tensor(w, w, clipped, ALU.mult).then_inc(masked_dve, 1)

            def max0(ph, t):
                wait_filled(dve, ph, "max0", t)
                dve.tensor_reduce(mx0[:, t:t + 1], misc_bank(ph, "max0", t)[:], AX.X,
                                  ALU.max).then_inc(misc_drained["dve"], 1)

            def mrow0(ph):
                wait_filled(dve, ph, "mrow0")
                dve.tensor_scalar(nm0[:], misc_bank(ph, "mrow0")[0:1, :], MAX_FLOOR, -1.0, ALU.max,
                                  ALU.mult).then_inc(misc_drained["dve"], 1)

            def max1(ph, g, n):
                t, h = divmod(n, PER_GROUP)
                wait_filled(dve, ph, "max1", g, n)
                dve.tensor_reduce(mx1[:, g, h, t:t + 1], misc_bank(ph, "max1", g, n)[:], AX.X,
                                  ALU.max, negate=True).then_inc(misc_drained["dve"], 1)

            def mrow1(ph, g):
                wait_filled(dve, ph, "mrow1", g)
                dve.tensor_copy(nm1[g][:], misc_bank(ph, "mrow1", g)[0:MAXIMA, 0:P])\
                   .then_inc(misc_drained["dve"], 1)

            def context0(ph, t):
                base = ph.j * FRONT_STEPS
                bank = misc_bank(ph, "context0", t)
                wait_filled(dve, ph, "context0", t)
                if t == 0:
                    dve.wait_ge(x_loaded, ph.j * DMA + DMA)
                dve.tensor_scalar(den0[:, t:t + 1], bank[:, D:D + 1], TINY, None, ALU.max).then_inc(front_step, 1)
                dve.wait_ge(front_step, base + 2 * t + 1)
                dve.reciprocal(rden0[:, t:t + 1], den0[:, t:t + 1]).then_inc(front_step, 1)
                dve.wait_ge(front_step, base + 2 * t + 2)
                dve.scalar_tensor_tensor(out=X[:, t, :], in0=bank[:, 0:D], scalar=rden0[:, t:t + 1],
                                         in1=X[:, t, :], op0=ALU.mult, op1=ALU.add)\
                   .then_inc(misc_drained["dve"], 1)
                wait_drained(dve, ph, "context0", t)
                dve.bn_stats(st0[:, t, :], X[:, t, :]).then_inc(stats_step, 1)

            def stats0(ph):
                dve.wait_ge(stats_step, ph.j * T + T)
                dve.memset(scratch[:], 0.0)
                for t in range(T):
                    dve.bn_aggr(mv0[:, t, :], st0[:, t, :]).then_inc(stats0_ready, 1)

            def norm0(ph):
                dve.wait_ge(rstd0_ready, ph.j + 1)
                if ph.back:
                    dve.wait_ge(res_ready, ph.i + 1)
                for t in range(T):
                    dve.tensor_scalar(xn[:, t, :], X[:, t, :], mv0[:, t, 0:1], rstd0[:, t:t + 1],
                                      ALU.subtract, ALU.mult).then_inc(xn_ready, 1)

            def reciprocal(ph, g, part):
                if part == 0:
                    dve.wait_ge(sums_out, (graph_of(ph, g) * GROUPS + g) * 2 + 2)
                q = slice(P * part, P * (part + 1))
                dve.reciprocal(sums_w[:, q], sums_w[:, q]).then_inc(back_step, 1)

            def normalise(ph, g):
                dve.wait_ge(back_step, graph_of(ph, g) * BACK_STEPS + (g + 1) * T)
                dve.tensor_tensor(sums_v[:], sums_v[:], sums_w[:], ALU.mult).then_inc(normalised, 1)

            def low_output(ph, g):
                dve.wait_ge(output_high, graph_of(ph, g) * GROUPS + g + 1)
                dve.tensor_tensor(OTL[:, g, :], sums_v[:], OTH[:, g, :].bitcast(F32),
                                  ALU.subtract).then_inc(output_low, 1)

            def add_residual(ph):
                dve.wait_ge(res_ready, ph.t + 1)
                dve.wait_ge(out_stored, ph.t * DMA + 1)
                for n, bank in enumerate((PV, DEN)):
                    dve.wait_ge(proj_filled, ph.t * 2 + n + 1)
                    dve.tensor_tensor(z[:, 2 * n:2 * n + 2, :], bank[:].rearrange("p (t e) -> p t e", t=2),
                                      res[:, 2 * n:2 * n + 2, :], ALU.add).then_inc(z_added, 1)

            def stats1(ph):
                dve.wait_ge(z_added, ph.t * 2 + 2)
                for t in range(T):
                    dve.bn_stats(st1[:, t, :], z[:, t, :]).then_inc(tail_step, 1)
                dve.wait_ge(tail_step, ph.t * T + T)
                dve.memset(scratch[:], 0.0)
                for t in range(T):
                    dve.bn_aggr(mv1[:, t, :], st1[:, t, :]).then_inc(stats1_ready, 1)

            def norm1(ph):
                dve.wait_ge(rstd1_ready, ph.t + 1)
                for t in range(T):
                    dve.tensor_scalar(z[:, t, :], z[:, t, :], mv1[:, t, 0:1], rstd1[:, t:t + 1],
                                      ALU.subtract, ALU.mult).then_inc(zn_ready, 1)

            do = {
                "prepare": prepare, "split": split, "clip": clip, "bias": bias,
                "q0": lambda ph, c: lo(ph, "q0", c, Q0L, Q0H, BQ0),
                "k0": lambda ph, c: lo(ph, "k0", c, K0L, K0H, BK0),
                "mask": mask, "max0": max0, "mrow0": mrow0, "context0": context0,
                "stats0": stats0, "norm0": norm0, "stats1": stats1,
                "transpose": xn_low,
                "q1": lambda ph, c: lo(ph, "q1", c, Q1L, Q1H, BQ1),
                "k1": lambda ph, c: lo(ph, "k1", c, K1L, K1H, BK1),
                "max1": max1, "mrow1": mrow1, "reciprocal": reciprocal, "normalise": normalise, "low_output": low_output,
                "project": add_residual,
                "norm1": norm1,
            }
            run(dve, lambda ph: follow(ph, do))

        @block.gpsimd
        def _(pool):
            POOL_STEPS0 = 1
            POOL_STEPS1 = 2

            pool.memset(z[:, 0, 0:1], 0.0).then_inc(out_stored, 1)
            pool.memset(ident[:], 0.0).then_inc(ident_zeroed, 1)
            pool.wait_ge(ident_zeroed, 1)
            pool.affine_select(out=ident[:], in_=ident[:], compare_op=ALU.not_equal, fill=1.0, base=0,
                               pattern=[[-1, P]], channel_multiplier=1).then_inc(ident_ready, 1)
            pool.wait_ge(consts_set, CONSTS)

            def prepare(ph, part):
                if part == 2:
                    pool.wait_ge(spread_ready, 4)

            def all_rows(n):
                return spread[:, n, :].unsqueeze(1).broadcast_to([P, T, D])

            def residual(ph):
                pool.wait_ge(xn_ready, ph.i * T + T)
                pool.tensor_tensor(res[:], xn[:], all_rows(S_G0), ALU.mult).then_inc(res_step, 1)
                pool.wait_ge(res_step, ph.i + 1)
                pool.tensor_tensor(res[:], res[:], all_rows(S_RES), ALU.add).then_inc(res_ready, 1)

            def rstd(var, ve, dst, step_sem, before, done):
                pool.tensor_tensor(ve[:], var, eps[:], ALU.add).then_inc(step_sem, 1)
                pool.wait_ge(step_sem, before + 1)
                pool.tensor_tensor(dst[:], ve[:], minus_half[:], ALU.pow).then_inc(done, 1)

            def mask(ph, quad, pair):
                if (quad, pair) in DVE_MASKS:
                    return
                if quad == 0 and pair == 0:
                    pool.wait_ge(adj_clipped, ph.i + 1)
                pool.wait_ge(exp_done, ph.i * TILES + PER_GROUP * quad + 2 * pair + 2)
                w, clipped = mask_operands(quad, pair)
                pool.tensor_tensor(w, w, clipped, ALU.mult).then_inc(masked_pool, 1)

            def rstd0_of(ph):
                pool.wait_ge(stats0_ready, ph.j * T + T)
                rstd(mv0[:, :, 1], ve0, rstd0, pool_step0, ph.j * POOL_STEPS0, rstd0_ready)

            def rstd1_of(ph):
                pool.wait_ge(stats1_ready, ph.t * T + T)
                rstd(mv1[:, :, 1], ve1, rstd1, pool_step1, ph.t * POOL_STEPS1, rstd1_ready)

            def output(ph):
                pool.wait_ge(zn_ready, ph.t * T + T)
                pool.tensor_tensor(z[:], z[:], all_rows(S_G1), ALU.mult).then_inc(pool_step1, 1)
                pool.wait_ge(pool_step1, ph.t * POOL_STEPS1 + 2)
                pool.tensor_tensor(z[:], z[:], all_rows(S_B1), ALU.add).then_inc(out_ready, 1)

            do = {"prepare": prepare, "residual": residual, "scores1": mask, "stats0": rstd0_of,
                  "stats1": rstd1_of, "output": output}
            run(pool, lambda ph: follow(ph, do))


def kernel(**inputs):
    import numpy as np
    import concourse.bacc as bacc
    from concourse.bass_utils import run_bass_kernel_spmd

    nc = bacc.Bacc("TRN2", target_bir_lowering=False, num_devices=1)
    arrays, args = {}, []

    def give(name, a):
        a = np.ascontiguousarray(a)
        arrays[name] = a
        args.append(nc.dram_tensor(name, a.shape, mybir.dt.from_np(a.dtype), kind="ExternalInput").ap())

    x, adj = np.asarray(inputs["x"]), np.asarray(inputs["adj"])
    give("x", x)
    give("x_t", x.transpose(0, 2, 1))
    give("adj_t", adj.transpose(0, 2, 1))
    for name in ("L0_gnn_Wq", "L0_gnn_Wk", "L0_gnn_Wc"):
        give(name, np.asarray(inputs[name]))
    for name in ("L1_gnn_Wq", "L1_gnn_Wk", "L1_gnn_Wv", "L1_gnn_Wo"):
        give(name, np.asarray(inputs[name]).T)
    cols = np.stack([np.asarray(inputs[name]) for name in COLS])
    give("channel_cols", cols.reshape(len(COLS), -1, P).transpose(2, 0, 1))
    give("channel_rows", np.stack([np.asarray(inputs[name]) for name in ROWS])[None])
    args.append(nc.dram_tensor("out", x.shape, mybir.dt.from_np(x.dtype), kind="ExternalOutput").ap())
    two_layer_graph_attention(nc, *args)
    r = run_bass_kernel_spmd(nc, [arrays], core_ids=[0])
    return r.results[0]["out"]
```
